# Optimizing a Trainium2 kernel written in Bass

```python
import numpy as np
import jax
import jax.numpy as jnp

def _softmax(x, axis=-1):
    return jax.nn.softmax(x, axis=axis)

def _gelu(x):
    return jax.nn.gelu(x, approximate=True)

def _silu(x):
    return jax.nn.silu(x)

def _sigmoid(x):
    return jax.nn.sigmoid(x)

def _layernorm(x, axis=-1, eps=1e-05):
    m = jnp.mean(x, axis=axis, keepdims=True)
    v = jnp.var(x, axis=axis, keepdims=True)
    return (x - m) / jnp.sqrt(v + eps)

def _scatter_add(tgt, idx, src, axis=0):
    return tgt.at[idx].add(src)

def _segment_sum(src, seg, n):
    return jax.ops.segment_sum(src, seg, n)
kernel_name = 'mk_sandwich_d1_jaxref_r4_e679bc'

def setup_inputs(seed: int=0):
    np.random.seed(seed)
    _w = jnp.asarray

    def _L0_attn_setup():
        import jax, jax.numpy as jnp
        import numpy as np
        HIDDEN = 512
        N_HEADS = 16
        HEAD_DIM = HIDDEN // N_HEADS
        BATCH = 2
        SEQ = 512
        key = jax.random.key(seed)
        ks = jax.random.split(key, 9)
        std = HIDDEN ** (-0.5)
        inp = {'hidden_states': jax.random.normal(ks[0], (BATCH, SEQ, HIDDEN), dtype=jnp.float32), 'q_w': jax.random.normal(ks[1], (HIDDEN, HIDDEN), dtype=jnp.float32) * std, 'k_w': jax.random.normal(ks[2], (HIDDEN, HIDDEN), dtype=jnp.float32) * std, 'v_w': jax.random.normal(ks[3], (HIDDEN, HIDDEN), dtype=jnp.float32) * std, 'o_w': jax.random.normal(ks[4], (HIDDEN, HIDDEN), dtype=jnp.float32) * std, 'q_b': jnp.zeros((HIDDEN,), dtype=jnp.float32), 'k_b': jnp.zeros((HIDDEN,), dtype=jnp.float32), 'v_b': jnp.zeros((HIDDEN,), dtype=jnp.float32), 'o_b': jnp.zeros((HIDDEN,), dtype=jnp.float32)}
        return inp
    _L0_attn_in = _L0_attn_setup()

    def _L0_ffn_setup():
        import jax, jax.numpy as jnp
        import numpy as np
        HIDDEN = 512
        INTER = 2048
        BATCH, LOCAL_SEQ = (2, 1024)
        key = jax.random.key(seed)
        k1, k2, k3 = jax.random.split(key, 3)
        h_shard = jax.random.normal(k1, (BATCH, LOCAL_SEQ, HIDDEN), dtype=jnp.float32)
        w_gate_up = jax.random.normal(k2, (2 * INTER, HIDDEN), dtype=jnp.float32) * 0.02
        w_down = jax.random.normal(k3, (HIDDEN, INTER), dtype=jnp.float32) * 0.02
        return {'h_shard': h_shard, 'w_gate_up': w_gate_up, 'w_down': w_down}
    _L0_ffn_in = _L0_ffn_setup()
    _d = {'L0_attn_hidden_states': _L0_attn_in['hidden_states'], 'L0_attn_q_w': _L0_attn_in['q_w'], 'L0_attn_k_w': _L0_attn_in['k_w'], 'L0_attn_v_w': _L0_attn_in['v_w'], 'L0_attn_o_w': _L0_attn_in['o_w'], 'L0_attn_q_b': _L0_attn_in['q_b'], 'L0_attn_k_b': _L0_attn_in['k_b'], 'L0_attn_v_b': _L0_attn_in['v_b'], 'L0_attn_o_b': _L0_attn_in['o_b'], 'L0_ffn_w_gate_up': _L0_ffn_in['w_gate_up'], 'L0_ffn_w_down': _L0_ffn_in['w_down']}
    _x0 = _d['L0_attn_hidden_states']
    _d['L0_attn_hidden_states'] = jax.random.normal(jax.random.fold_in(jax.random.key(seed), 1), (2, 1024, 512), dtype=_x0.dtype)
    del _x0
    return _d

def reference(L0_attn_hidden_states, L0_attn_q_w, L0_attn_k_w, L0_attn_v_w, L0_attn_o_w, L0_attn_q_b, L0_attn_k_b, L0_attn_v_b, L0_attn_o_b, L0_ffn_w_gate_up, L0_ffn_w_down):

    def _L0_attn_ref(hidden_states, q_w, k_w, v_w, o_w, q_b, k_b, v_b, o_b):
        import jax, jax.numpy as jnp
        import numpy as np
        HIDDEN = 512
        N_HEADS = 16
        HEAD_DIM = HIDDEN // N_HEADS
        BATCH = 2
        SEQ = 512
        b, s, _ = hidden_states.shape

        def proj(w, bias):
            y = hidden_states @ w.T + bias
            return y.reshape(b, s, N_HEADS, HEAD_DIM).transpose(0, 2, 1, 3)
        q = proj(q_w, q_b)
        k = proj(k_w, k_b)
        v = proj(v_w, v_b)
        scale = 1.0 / jnp.sqrt(jnp.float32(HEAD_DIM))
        scores = jnp.einsum('bhqd,bhkd->bhqk', q, k) * scale
        qi = jnp.arange(s)[:, None]
        ki = jnp.arange(s)[None, :]
        scores = jnp.where(ki > qi, -jnp.inf, scores)
        attn = jax.nn.softmax(scores.astype(jnp.float32), axis=-1).astype(q.dtype)
        out = jnp.einsum('bhqk,bhkd->bhqd', attn, v)
        out = out.transpose(0, 2, 1, 3).reshape(b, s, HIDDEN)
        return out @ o_w.T + o_b

    def _L0_ffn_ref(h_shard, w_gate_up, w_down):
        import jax, jax.numpy as jnp
        import numpy as np
        HIDDEN = 512
        INTER = 2048
        BATCH, LOCAL_SEQ = (2, 1024)
        batch, local_seq, hidden = h_shard.shape
        gate_up = jnp.einsum('bsh,oh->bso', h_shard, w_gate_up)
        gate, up = jnp.split(gate_up, 2, axis=-1)
        h = jax.nn.silu(gate) * up
        out = jnp.einsum('bsi,hi->bsh', h, w_down)
        return out
    x = L0_attn_hidden_states
    x = x + _layernorm(_L0_attn_ref(_layernorm(x, axis=-1), L0_attn_q_w, L0_attn_k_w, L0_attn_v_w, L0_attn_o_w, L0_attn_q_b, L0_attn_k_b, L0_attn_v_b, L0_attn_o_b), axis=-1)
    x = x + _layernorm(_L0_ffn_ref(_layernorm(x, axis=-1), L0_ffn_w_gate_up, L0_ffn_w_down), axis=-1)
    return x

_drawn_inputs = setup_inputs


def setup_inputs(seed=0):
    import zlib

    import numpy as np

    out = dict(_drawn_inputs(seed))
    spreads = {'L0_attn_q_b': (0.0, 0.1),
     'L0_attn_k_b': (0.0, 0.1),
     'L0_attn_v_b': (0.0, 0.1),
     'L0_attn_o_b': (0.0, 0.1)}
    factors = {}
    for name, (base, spread) in spreads.items():
        noise = np.random.default_rng([zlib.crc32(name.encode()), seed]).standard_normal(out[name].shape)
        drawn = base * np.exp(spread * noise) if base else spread * noise
        out[name] = jnp.asarray(drawn.astype(out[name].dtype))
    for name, factor in factors.items():
        out[name] = (out[name] * factor).astype(out[name].dtype)
    return out
```

```python
import concourse.bass as bass
from concourse import mybir
from contextlib import ExitStack

import numpy as np

F32 = mybir.dt.float32
F32R = mybir.dt.float32r
BF16 = mybir.dt.bfloat16
ALU = mybir.AluOpType
ACT = mybir.ActivationFunctionType
AX = mybir.AxisListType

P = 128
BATCH, SEQ, HID = 2, 1024, 512
HEADS, HD = 16, 32
INTER = 2048
KT = HID // P
TT = SEQ // P
CH = 512
NCH = SEQ // CH
UNITS = HEADS // 2
QK_ROWS = 3 * HD
ROWS = QK_ROWS + 2
SCALE = float(1.0 / np.sqrt(np.float32(HD)))
MASKED = -1.0e30
EPS = 1e-5
RING = 4
DMA = 16

CHUNKS = INTER // P
BLK = 512
BLOCKS = BATCH * SEQ // BLK
BT = BLK // P
GU = 2 * P

STEPS = [(c, kt, max(0, kt * P - c * CH)) for c in range(NCH) for kt in range((c + 1) * CH // P)]
NST = len(STEPS)
CHUNK_END = [max(j for j, s in enumerate(STEPS) if s[0] == c) for c in range(NCH)]
MAXES = [(h, t, half) for h in range(2) for t in range(TT) for half in range(t * P // CH + 1)]
NMAX = len(MAXES)
MAX_FROM = 4
STACK_DMAS = NCH * 2 * 6

MT = 2 * NCH
PER_UNIT = NMAX + MT + NCH
USE_XT = 0
USE_V = USE_XT + TT
USE_PROJ0 = USE_V + TT
USE_MAX0 = USE_PROJ0 + NCH
USE_MT0 = USE_MAX0 + NMAX
USE_PROJ1 = USE_MT0 + MT
USE_BODY = USE_PROJ1 + NCH
USE_O = USE_BODY + (UNITS - 2) * PER_UNIT + NMAX + MT
PER_BATCH = USE_O + 2 * TT
NORMS = 3 * TT
assert (2 * PER_UNIT) % RING == 0


def use_of_proj(u):
    return USE_PROJ0 if u == 0 else USE_PROJ1 + (u - 1) * PER_UNIT


def use_of_o(t):
    return USE_O + (0 if t == 0 else 2 * t - 1)


def use_of_xt2(t):
    return USE_O + (2 * t + 2 if t < TT - 1 else 2 * TT - 1)


def at(const, per, i):
    return const if i is None else i * per + const


def build(nc, x, qk_w, v_w, o_w, v_b, o_b, gu_w, dn_w, x1_dram, out):
    ctx = ExitStack()
    with ctx:
        def sb(stack, name, shape, dt=F32):
            return stack.enter_context(nc.sbuf_tensor(name, shape, dt))

        def sem(name):
            return ctx.enter_context(nc.semaphore(name))

        xt_hi = sb(ctx, "xt_hi", [P, BATCH, KT, SEQ], F32R)
        xt_lo = sb(ctx, "xt_lo", [P, BATCH, KT, SEQ], F32R)
        ident = sb(ctx, "ident", [P, P])
        ident_bf = sb(ctx, "ident_bf", [P, P], BF16)
        mask_q = sb(ctx, "mask_q", [P, P], BF16)
        mask_k = sb(ctx, "mask_k", [P, P], BF16)
        ones = sb(ctx, "ones", [P, HD])
        eps = sb(ctx, "eps", [P, 1])
        stats = sb(ctx, "stats", [P, BT, 6])
        mv = sb(ctx, "mv", [P, BT, 2])
        std = sb(ctx, "std", [P, BT])
        rstd = sb(ctx, "rstd", [P, BT])
        x_in = sb(ctx, "x_in", [P, 2, HID])
        y = sb(ctx, "y", [P, HID])
        x1 = sb(ctx, "x1", [P, 2, HID])

        att = ExitStack()
        with att:
            q_stack = sb(att, "q_stack", [P, 2, 2, SEQ], F32R)
            k_stack = sb(att, "k_stack", [P, 2, 2, SEQ], F32R)
            st_hi = sb(att, "st_hi", [P, NCH, CH], F32R)
            st_lo = sb(att, "st_lo", [P, NCH, CH], F32R)
            probs = sb(att, "probs", [P, 2, 2, CH])
            qk_raw = sb(att, "qk_raw", [P, 2, KT * P + 1])
            qk_hi = sb(att, "qk_hi", [P, 2, KT, P], F32R)
            qk_lo = sb(att, "qk_lo", [P, 2, KT, P], F32R)
            vo_raw = sb(att, "vo_raw", [P, KT, HID])
            vo_hi = sb(att, "vo_hi", [P, KT, HID], F32R)
            vo_lo = sb(att, "vo_lo", [P, KT, HID], F32R)
            v = sb(att, "v", [P, TT, HID])
            v_pair = sb(att, "v_pair", [P, 2, TT, 2 * HD])
            attn = sb(att, "attn", [P, KT, SEQ])
            rec = sb(att, "rec", [2 * HD, CH])
            xn = sb(att, "xn", [P, 2, HID])
            v_bias = sb(att, "v_bias", [P, HID])
            o_bias = sb(att, "o_bias", [P, HID])
            m_part = sb(att, "m_part", [P, 2, TT // 2, 2])
            m_full = sb(att, "m_full", [P, 2, TT])
            m_cols = sb(att, "m_cols", [P, 2, TT, 2], F32R)
        ffn = ExitStack()
        with ffn:
            gu_raw = sb(ffn, "gu_raw", [P, 2, KT * GU])
            gu_hi = sb(ffn, "gu_hi", [P, 2, KT * GU], F32R)
            gu_lo = sb(ffn, "gu_lo", [P, 2, KT * GU], F32R)
            dn_raw = sb(ffn, "dn_raw", [P, 2, HID])
            dn_hi = sb(ffn, "dn_hi", [P, 2, HID], F32R)
            dn_lo = sb(ffn, "dn_lo", [P, 2, HID], F32R)
            silu = sb(ffn, "silu", [P, 2, BLK])
            h32 = sb(ffn, "h32", [P, 2, BLK])
            h_hi = sb(ffn, "h_hi", [P, 2, BLK], F32R)
            h_lo = sb(ffn, "h_lo", [P, 2, BLK], F32R)
            out_t = sb(ffn, "out_t", [P, 2, HID])
        ps = ctx.enter_context(nc.psum_tensor("ps", [P, 8, CH], F32))
        ST_BANK, ACC_BANK = RING, RING + 2
        G_BANK, U_BANK = 4, 6

        consts_loaded = sem("consts_loaded")
        consts_made = sem("consts_made")
        x_loaded = [sem(f"x_loaded{s}") for s in range(2)]
        xn_ready = sem("xn_ready")
        x1_ready = sem("x1_ready")
        x1_stored = [sem(f"x1_stored{s}") for s in range(2)]
        vo_loaded = sem("vo_loaded")
        vo_split = sem("vo_split")
        qk_loaded = [sem(f"qk_loaded{s}") for s in range(2)]
        qk_split = sem("qk_split")
        pool_hi = sem("pool_hi")
        bank_full = sem("bank_full")
        bank_free = sem("bank_free")
        hi_ready = sem("hi_ready")
        v_paired = sem("v_paired")
        stack_loaded = [sem(f"stack_loaded{s}") for s in range(2)]
        m_ready = sem("m_ready")
        score_full = sem("score_full")
        p_ready = sem("p_ready")
        p_used = sem("p_used")
        acc_free = sem("acc_free")
        attn_split = sem("attn_split")
        var_ready = sem("var_ready")
        std_ready = sem("std_ready")
        dve = sem("dve")
        dve_unit = sem("dve_unit")
        qk_hi_done = sem("qk_hi_done")
        gu_hi_done = sem("gu_hi_done")
        dn_hi_done = sem("dn_hi_done")
        gu_loaded = [sem(f"gu_loaded{s}") for s in range(2)]
        dn_loaded = [sem(f"dn_loaded{s}") for s in range(2)]
        gu_split = sem("gu_split")
        dn_split = sem("dn_split")
        gu_full = sem("gu_full")
        silu_ready = sem("silu_ready")
        h_part = sem("h_part")
        h_ready = sem("h_ready")
        down_done = sem("down_done")
        acc_out = sem("acc_out")
        out_ready = sem("out_ready")
        acc_half = sem("acc_half")
        out_stored = [sem(f"out_stored{s}") for s in range(2)]

        block = ctx.enter_context(nc.Block())

        def unit_no(b, u):
            return b * UNITS + u

        @block.sync
        def _(sp):
            sp.dma_start(v_bias[:, :], v_b.partition_broadcast(P)).then_inc(consts_loaded, DMA)
            sp.dma_start(o_bias[:, :], o_b.partition_broadcast(P)).then_inc(consts_loaded, DMA)

            def load_x(e, src):
                if e >= 2:
                    turn, t = divmod(e - 2, TT)
                    if turn >= 2 * BATCH:
                        sp.wait_ge(out_ready, e - 2 - 2 * BATCH * TT + 1)
                    elif turn % 2:
                        sp.wait_ge(x1_ready, turn // 2 * TT + t + 1)
                    else:
                        sp.wait_ge(xn_ready, e - 1)
                sp.dma_start(x_in[:, e % 2, :], src).then_inc(x_loaded[e % 2], DMA)

            def load_qk(b, u, i=None):
                g = unit_no(b, u)
                if i is not None:
                    sp.wait_ge(bank_free, at(b * PER_BATCH + USE_PROJ1 + (u - 3) * PER_UNIT + NCH, 2 * PER_UNIT, i))
                elif b:
                    sp.wait_ge(bank_free, (b - 1) * PER_BATCH + use_of_proj(UNITS - 2 + u) + NCH)
                src = qk_w[u] if i is None else qk_w[bass.ds(i * 2 + u, 1)].rearrange("a p n -> (a p) n")
                sp.dma_start(qk_raw[:, g % 2, :], src).then_inc(qk_loaded[g % 2], DMA)

            def load_stacks(b, u, use, i=None):
                g = unit_no(b, u)
                s = g % 2
                for c in range(NCH):
                    sp.wait_ge(bank_free, at(use + c + 1, 2 * PER_UNIT, i))
                    cols = slice(c * CH, (c + 1) * CH)
                    for h in range(2):
                        q, k = slice(h * HD, (h + 1) * HD), slice((2 + h) * HD, (3 + h) * HD)
                        for stack, rows, part in ((q_stack, q, (st_hi, st_lo, st_hi)), (k_stack, k, (st_hi, st_hi, st_lo))):
                            for n, src in enumerate(part):
                                sp.dma_start(stack[n * HD:(n + 1) * HD, s, h, cols].bitcast(F32), src[rows, c, :].bitcast(F32)).then_inc(stack_loaded[s], DMA)

            for b in range(BATCH):
                base = b * PER_BATCH
                for t in range(TT):
                    load_x(b * 2 * TT + t, x[(b * TT + t) * P:(b * TT + t + 1) * P, :])
                    if t == 1:
                        if b:
                            sp.wait_ge(vo_split, 2 * b)
                        sp.dma_start(vo_raw[:, :, :], v_w).then_inc(vo_loaded, DMA)
                        load_qk(b, 0)
                        load_qk(b, 1)
                sp.wait_ge(vo_split, 2 * b + 1)
                sp.dma_start(vo_raw[:, :, :], o_w).then_inc(vo_loaded, DMA)
                load_stacks(b, 0, base + USE_PROJ0)
                load_stacks(b, 1, base + USE_PROJ1)
                with sp.Fori(0, UNITS // 2 - 1) as i:
                    for s in range(2):
                        body = base + USE_BODY + s * PER_UNIT
                        load_qk(b, s + 2, i)
                        load_stacks(b, s + 2, body + NMAX + MT, i)
                for t in range(TT + 1):
                    if t < TT:
                        load_x(b * 2 * TT + TT + t, x[(b * TT + t) * P:(b * TT + t + 1) * P, :])
                    if t:
                        e = b * TT + t - 1
                        sp.wait_ge(x1_ready, e + 1)
                        sp.dma_start(x1_dram[e * P:(e + 1) * P, :], x1[:, e % 2, :]).then_inc(x1_stored[e % 2], DMA)

            def load_w(n, c, i=None):
                s = n % 2
                gu, dn = (gu_w[c], dn_w[c]) if i is None else \
                    [w[bass.ds(i * 2 + c, 1)].rearrange("a p n -> (a p) n") for w in (gu_w, dn_w)]
                if n >= 2:
                    sp.wait_ge(gu_split, at(n - 1, 2, i))
                sp.dma_start(gu_raw[:, s], gu).then_inc(gu_loaded[s], DMA)
                if n >= 2:
                    sp.wait_ge(dn_split, at(n - 1, 2, i))
                sp.dma_start(dn_raw[:, s], dn).then_inc(dn_loaded[s], DMA)

            for s in range(2):
                sp.wait_ge(x1_stored[s], DMA * BATCH * TT // 2)

            def finish(blk):
                for t in range(BT):
                    e = blk * BT + t
                    load_x(2 * BATCH * TT + e, x1_dram[e * P:(e + 1) * P, :])
                for t in range(BT):
                    e = blk * BT + t
                    sp.wait_ge(out_ready, e + 1)
                    sp.dma_start(out[e * P:(e + 1) * P, :], out_t[:, e % 2, :]).then_inc(out_stored[e % 2], DMA)

            for blk in range(BLOCKS):
                n0 = blk * CHUNKS
                for c in range(4):
                    load_w(n0 + c, c)
                if blk:
                    finish(blk - 1)
                with sp.Fori(0, CHUNKS // 2 - 2) as i:
                    load_w(n0 + 4, 4, i)
                    load_w(n0 + 5, 5, i)
            finish(BLOCKS - 1)
            for s in range(2):
                sp.wait_ge(out_stored[s], DMA * BLOCKS * BT // 2)

        @block.gpsimd
        def _(pool):
            nc.gpsimd.memset(ident[:, :], 0.0).then_inc(pool_hi, 1)
            nc.gpsimd.memset(mask_q[:, :], 0.0).then_inc(pool_hi, 1)
            nc.gpsimd.memset(mask_k[:, :], 0.0).then_inc(pool_hi, 1)
            nc.gpsimd.memset(ones[:, :], 1.0).then_inc(pool_hi, 1)
            nc.gpsimd.memset(eps[:, :], EPS).then_inc(pool_hi, 1)
            pool.wait_ge(pool_hi, 5)
            nc.gpsimd.memset(k_stack[QK_ROWS:ROWS, :, :, :].bitcast(F32), 1.0).then_inc(pool_hi, 1)
            pool.wait_ge(pool_hi, 6)
            nc.gpsimd.affine_select(out=ident[:, :], in_=ident[:, :], compare_op=ALU.not_equal, fill=1.0,
                                    base=0, pattern=[[-1, P]], channel_multiplier=1).then_inc(pool_hi, 1)
            nc.gpsimd.affine_select(out=mask_q[:, :], in_=mask_q[:, :], compare_op=ALU.is_ge, fill=MASKED,
                                    base=0, pattern=[[-1, P]], channel_multiplier=1).then_inc(pool_hi, 1)
            nc.gpsimd.affine_select(out=mask_k[:, :], in_=mask_k[:, :], compare_op=ALU.is_ge, fill=MASKED,
                                    base=0, pattern=[[1, P]], channel_multiplier=-1).then_inc(pool_hi, 1)
            pool.wait_ge(pool_hi, 9)
            nc.gpsimd.tensor_copy(ident_bf[:, :], ident[:, :]).then_inc(consts_made, 1)
            made = [9]

            def split(hi, lo, raw, done):
                nc.gpsimd.tensor_copy(hi, raw).then_inc(pool_hi, 1)
                made[0] += 1
                pool.wait_ge(pool_hi, made[0])
                nc.gpsimd.tensor_tensor(lo, raw, hi.bitcast(F32), ALU.subtract).then_inc(done, 1)

            def qk_rest(b, u, i=None):
                g = unit_no(b, u)
                pool.wait_ge(qk_hi_done, at(g + 1, 2, i))
                nc.gpsimd.tensor_tensor(qk_lo[:, g % 2], qk_raw[:, g % 2, 0:KT * P], qk_hi[:, g % 2].bitcast(F32),
                                        ALU.subtract).then_inc(qk_split, 1)

            def pair_values(b, u, i=None):
                g = unit_no(b, u)
                if g >= 2:
                    pool.wait_ge(p_used, at(NST * (g - 1), 2 * NST, i))
                cols = bass.ds(i * (4 * HD) + u * 2 * HD, 2 * HD) if i is not None else slice(u * 2 * HD, (u + 1) * 2 * HD)
                nc.gpsimd.tensor_copy(v_pair[:, g % 2], v[:, :, cols]).then_inc(v_paired, 1)

            for b in range(BATCH):
                base = b * PER_BATCH
                pool.wait_ge(vo_loaded, DMA * (2 * b + 1))
                if b:
                    pool.wait_ge(bank_full, (b - 1) * PER_BATCH + PER_BATCH)
                split(vo_hi[:, :, :], vo_lo[:, :, :], vo_raw[:, :, :], vo_split)
                for u in range(2):
                    qk_rest(b, u)
                pool.wait_ge(bank_free, base + USE_V + TT)
                pair_values(b, 0)
                pool.wait_ge(vo_loaded, DMA * (2 * b + 2))
                split(vo_hi[:, :, :], vo_lo[:, :, :], vo_raw[:, :, :], vo_split)
                with pool.Fori(0, UNITS // 2 - 1) as i:
                    for s in range(2):
                        qk_rest(b, s + 2, i)
                        pair_values(b, s + 1, i)
                pair_values(b, UNITS - 1)
                pool.wait_ge(bank_full, base + use_of_proj(UNITS - 1) + NCH)
                for k in range(KT):
                    pool.wait_ge(acc_free, 2 * NCH * (unit_no(b, 0) // 2 + k + 1))
                    split(xt_hi[:, b, k, :], xt_lo[:, b, k, :], attn[:, k, :], attn_split)

            def gu_rest(n, i=None):
                s = n % 2
                pool.wait_ge(gu_hi_done, at(n + 1, 2, i))
                nc.gpsimd.tensor_tensor(gu_lo[:, s], gu_raw[:, s], gu_hi[:, s].bitcast(F32), ALU.subtract).then_inc(gu_split, 1)

            def dn_rest(n, i=None):
                s = n % 2
                pool.wait_ge(dn_hi_done, at(n + 1, 2, i))
                nc.gpsimd.tensor_tensor(dn_lo[:, s], dn_raw[:, s], dn_hi[:, s].bitcast(F32), ALU.subtract).then_inc(dn_split, 1)

            gu_rest(0)
            gu_rest(1)
            dn_rest(0)
            with pool.Fori(0, BLOCKS * CHUNKS // 2 - 1) as i:
                for s in range(2):
                    gu_rest(s + 2, i)
                    dn_rest(s + 1, i)
            dn_rest(BLOCKS * CHUNKS - 1)

        @block.scalar
        def _(act):
            def root(n):
                tiles = 1 if n < BATCH * NORMS else BT
                act.wait_ge(var_ready, n + 1 if tiles == 1 else BATCH * NORMS + BT * (n + 1 - BATCH * NORMS))
                nc.scalar.activation(std[:, 0:tiles], mv[:, 0:tiles, 1], ACT.Sqrt, bias=eps[:, :]).then_inc(std_ready, 1)

            def hi_of_xt(b, t, use):
                act.wait_ge(bank_full, use + 1)
                nc.scalar.activation(xt_hi[:, b, :, t * P:(t + 1) * P], ps[:, use % RING].rearrange("p (k c) -> p k c", k=KT),
                                     ACT.Copy).then_inc(hi_ready, 1)

            def hi_of_proj(b, u, use, i=None):
                g = unit_no(b, u)
                for c in range(NCH):
                    act.wait_ge(bank_full, at(use + c + 1, 2 * PER_UNIT, i))
                    if g >= 1:
                        act.wait_ge(stack_loaded[(g - 1) % 2], at(DMA * STACK_DMAS * ((g - 1) // 2 + 1), DMA * STACK_DMAS, i))
                    nc.scalar.activation(st_hi[:, c, :], ps[:, (use + c) % RING], ACT.Identity, bias=qk_raw[:, g % 2, KT * P:]).then_inc(hi_ready, 1)

            def hi_of_qk(b, u, i=None):
                g = unit_no(b, u)
                s = g % 2
                act.wait_ge(qk_loaded[s], at(DMA * (g // 2 + 1), DMA, i))
                nc.scalar.activation(qk_hi[:, s].rearrange("p k n -> p (k n)"), qk_raw[:, s, 0:KT * P], ACT.Copy).then_inc(qk_hi_done, 1)

            def exps(b, u, i=None):
                g = unit_no(b, u)
                for j, (c, kt, off) in enumerate(STEPS):
                    for h in range(2):
                        act.wait_ge(score_full, at(2 * NST * g + 2 * j + h + 1, 4 * NST, i))
                        if g * NST + j >= 2 and h == 0:
                            act.wait_ge(p_used, at(NST * g + j - 1, 2 * NST, i))
                        nc.scalar.activation(probs[:, j % 2, h, 0:CH - off], ps[:, ST_BANK + h, 0:CH - off], ACT.Exp,
                                             scale=SCALE).then_inc(p_ready, 1)

            act.wait_ge(consts_loaded, 2 * DMA)
            act.wait_ge(consts_made, 1)
            for b in range(BATCH):
                base = b * PER_BATCH
                for t in range(TT + 1):
                    if t < TT:
                        root(b * NORMS + t)
                    if t:
                        hi_of_xt(b, t - 1, base + USE_XT + t - 1)
                for u in range(2):
                    hi_of_qk(b, u)
                for u in range(2):
                    hi_of_proj(b, u, base + use_of_proj(u))
                with act.Fori(0, UNITS // 2 - 1) as i:
                    for s in range(2):
                        hi_of_qk(b, s + 2, i)
                        exps(b, s, i)
                        hi_of_proj(b, s + 2, base + USE_BODY + s * PER_UNIT + NMAX + MT, i)
                for u in (UNITS - 2, UNITS - 1):
                    exps(b, u)
                for t in range(TT + 1):
                    if t < TT:
                        root(b * NORMS + TT + 2 * t)
                        root(b * NORMS + TT + 2 * t + 1)
                    if t:
                        hi_of_xt(b, t - 1, base + use_of_xt2(t - 1))

            def silus(n, i=None):
                s = n % 2
                act.wait_ge(gu_full, at(2 * n + 1, 4, i))
                if n >= 2:
                    act.wait_ge(h_ready, at(n - 1, 2, i))
                nc.scalar.activation(silu[:, s, :], ps[:, G_BANK + s], ACT.Silu).then_inc(silu_ready, 1)

            def hi_of_gu(n, i=None):
                s = n % 2
                act.wait_ge(gu_loaded[s], at(DMA * (n // 2 + 1), DMA, i))
                if n >= 2:
                    act.wait_ge(gu_full, at(2 * n - 2, 4, i))
                nc.scalar.activation(gu_hi[:, s], gu_raw[:, s], ACT.Copy).then_inc(gu_hi_done, 1)

            def hi_of_dn(n, i=None):
                s = n % 2
                act.wait_ge(dn_loaded[s], at(DMA * (n // 2 + 1), DMA, i))
                if n >= 2:
                    act.wait_ge(down_done, at(n - 1, 2, i))
                nc.scalar.activation(dn_hi[:, s], dn_raw[:, s], ACT.Copy).then_inc(dn_hi_done, 1)

            def chunk(n, i=None):
                silus(n, i)
                if n < BLOCKS * CHUNKS - 2:
                    hi_of_gu(n + 2, i)
                if n < BLOCKS * CHUNKS - 1:
                    hi_of_dn(n + 1, i)

            hi_of_gu(0)
            hi_of_gu(1)
            hi_of_dn(0)
            for blk in range(BLOCKS):
                n0 = blk * CHUNKS
                chunk(n0)
                if blk:
                    root(BATCH * NORMS + blk - 1)
                chunk(n0 + 1)
                with act.Fori(0, CHUNKS // 2 - 2) as i:
                    chunk(n0 + 2, i)
                    chunk(n0 + 3, i)
                chunk(n0 + CHUNKS - 2)
                chunk(n0 + CHUNKS - 1)
            root(BATCH * NORMS + BLOCKS - 1)

        @block.vector
        def _(vec):
            n_dve = [0]

            def step(ins):
                n_dve[0] += 1
                ins.then_inc(dve, 1)
                vec.wait_ge(dve, n_dve[0])

            def moments(src, n):
                step(nc.vector.bn_stats(stats[:, 0, :], src))
                nc.vector.bn_aggr(mv[:, 0, :], stats[:, 0, :]).then_inc(var_ready, 1)
                vec.wait_ge(std_ready, n + 1)
                step(nc.vector.reciprocal(rstd[:, 0:1], std[:, 0:1]))

            def normed(dst, src):
                return nc.vector.tensor_scalar(dst, src, mv[:, 0, 0:1], rstd[:, 0:1], ALU.subtract, ALU.mult)

            def norm_x(b, t):
                e = b * 2 * TT + t
                vec.wait_ge(x_loaded[e % 2], DMA * (e // 2 + 1))
                moments(x_in[:, e % 2, :], b * NORMS + t)
                normed(xn[:, e % 2, :], x_in[:, e % 2, :]).then_inc(xn_ready, 1)

            def lo_of_xt(b, t, use, n):
                vec.wait_ge(hi_ready, n + 1)
                cols = slice(t * P, (t + 1) * P)
                nc.vector.tensor_tensor(xt_lo[:, b, :, cols], ps[:, use % RING].rearrange("p (k c) -> p k c", k=KT),
                                        xt_hi[:, b, :, cols].bitcast(F32), ALU.subtract).then_inc(bank_free, 1)

            HI = 2 * TT + UNITS * NCH

            def lo_of_proj(b, u, use, i=None):
                g = unit_no(b, u)
                for c in range(NCH):
                    vec.wait_ge(hi_ready, at(b * HI + TT + u * NCH + c + 1, 2 * NCH, i))
                    nc.vector.scalar_tensor_tensor(st_lo[:, c, :], ps[:, (use + c) % RING], qk_raw[:, g % 2, KT * P:], st_hi[:, c, :].bitcast(F32),
                                                   ALU.add, ALU.subtract).then_inc(bank_free, 1)

            def maxima(b, u, use, i=None):
                g = unit_no(b, u)
                for n, (h, t, half) in enumerate(MAXES):
                    width = min(CH, (t + 1) * P - half * CH)
                    dst = m_full[:, h, t:t + 1] if t < TT // 2 else m_part[:, h, t - TT // 2, half:half + 1]
                    vec.wait_ge(bank_full, at(use + n + 1, 2 * PER_UNIT, i))
                    nc.vector.reduce_max(dst, ps[:, (use + n) % RING, 0:width], AX.X).then_inc(bank_free, 1)
                vec.wait_ge(bank_free, at(use + NMAX, 2 * PER_UNIT, i))
                nc.vector.reduce_max(m_full[:, :, TT // 2:TT], m_part[:, :, :, :], AX.X).then_inc(dve_unit, 1)
                vec.wait_ge(dve_unit, at(2 * g + 1, 4, i))
                nc.vector.tensor_scalar(m_cols[:, :, :, 0], m_full[:, :, :], -1.0, None, ALU.mult).then_inc(dve_unit, 1)
                vec.wait_ge(dve_unit, at(2 * g + 2, 4, i))
                nc.vector.scalar_tensor_tensor(m_cols[:, :, :, 1], m_full[:, :, :], -1.0, m_cols[:, :, :, 0].bitcast(F32),
                                               ALU.mult, ALU.subtract).then_inc(m_ready, 1)

            def max_rows(b, u, use, i=None):
                g = unit_no(b, u)
                for n in range(MT):
                    h, c = divmod(n, NCH)
                    vec.wait_ge(bank_full, at(use + n + 1, 2 * PER_UNIT, i))
                    nc.vector.tensor_copy(q_stack[QK_ROWS:ROWS, g % 2, h, c * CH:(c + 1) * CH], ps[0:2, (use + n) % RING]).then_inc(bank_free, 1)

            def normalise(b, u, c, i=None):
                g = unit_no(b, u)
                vec.wait_ge(p_used, at(NST * g + CHUNK_END[c] + 1, 2 * NST, i))
                if NCH * g + c:
                    vec.wait_ge(acc_free, at(NCH * g + c, 2 * NCH, i))
                nc.vector.reciprocal(rec[:, :], ps[2 * HD:4 * HD, ACC_BANK + c]).then_inc(acc_half, 1)
                vec.wait_ge(acc_half, at(NCH * g + c + 1, 2 * NCH, i))
                rows = slice((u % 2) * 2 * HD, (u % 2 + 1) * 2 * HD)
                dst = attn[rows, u // 2, c * CH:(c + 1) * CH] if i is None else \
                    attn[rows, bass.ds(i + u // 2, 1), c * CH:(c + 1) * CH].rearrange("p a c -> p (a c)")
                nc.vector.tensor_tensor(dst, ps[0:2 * HD, ACC_BANK + c], rec[:, :], ALU.mult).then_inc(acc_free, 1)

            vec.wait_ge(consts_loaded, 2 * DMA)
            for b in range(BATCH):
                base = b * PER_BATCH
                for t in range(TT + 1):
                    if t < TT:
                        norm_x(b, t)
                    if t:
                        lo_of_xt(b, t - 1, base + USE_XT + t - 1, b * HI + t - 1)
                for t in range(TT):
                    use = base + USE_V + t
                    vec.wait_ge(bank_full, use + 1)
                    nc.vector.tensor_tensor(v[:, t, :], ps[:, use % RING], v_bias[:, :], ALU.add).then_inc(bank_free, 1)
                lo_of_proj(b, 0, base + USE_PROJ0)
                maxima(b, 0, base + USE_MAX0)
                max_rows(b, 0, base + USE_MT0)
                lo_of_proj(b, 1, base + USE_PROJ1)

                def body(u, use, i, project):
                    normalise(b, u, 0, i)
                    maxima(b, u + 1, use, i)
                    max_rows(b, u + 1, use + NMAX, i)
                    normalise(b, u, 1, i)
                    if project:
                        lo_of_proj(b, u + 2, use + NMAX + MT, i)

                with vec.Fori(0, UNITS // 2 - 1) as i:
                    for s in range(2):
                        body(s, base + USE_BODY + s * PER_UNIT, i, True)
                body(UNITS - 2, base + USE_BODY + (UNITS - 2) * PER_UNIT, None, False)
                for c in range(NCH):
                    normalise(b, UNITS - 1, c)

                for t in range(TT + 1):
                    if t < TT:
                        e = b * TT + t
                        ex = b * 2 * TT + TT + t
                        use = base + use_of_o(t)
                        vec.wait_ge(bank_full, use + 1)
                        nc.vector.tensor_tensor(y[:, :], ps[:, use % RING], o_bias[:, :], ALU.add).then_inc(bank_free, 1)
                        vec.wait_ge(bank_free, use + 1)
                        moments(y[:, :], b * NORMS + TT + 2 * t)
                        step(normed(y[:, :], y[:, :]))
                        vec.wait_ge(x_loaded[ex % 2], DMA * (ex // 2 + 1))
                        if e >= 2:
                            vec.wait_ge(x1_stored[e % 2], DMA * (e // 2))
                        nc.vector.tensor_tensor(x1[:, e % 2, :], x_in[:, ex % 2, :], y[:, :], ALU.add).then_inc(x1_ready, 1)
                        vec.wait_ge(x1_ready, e + 1)
                        moments(x1[:, e % 2, :], b * NORMS + TT + 2 * t + 1)
                        nc.vector.tensor_scalar(xn[:, t % 2, :], x1[:, e % 2, :], mv[:, 0, 0:1], rstd[:, 0:1],
                                                ALU.subtract, ALU.mult).then_inc(xn_ready, 1)
                    if t:
                        lo_of_xt(b, t - 1, base + use_of_xt2(t - 1), b * HI + TT + UNITS * NCH + t - 1)

            def hidden(n, i=None):
                s = n % 2
                vec.wait_ge(silu_ready, at(n + 1, 2, i))
                vec.wait_ge(gu_full, at(2 * n + 2, 4, i))
                nc.vector.tensor_tensor(h32[:, s, :], ps[:, U_BANK + s], silu[:, s, :], ALU.mult).then_inc(h_part, 1)
                vec.wait_ge(h_part, at(2 * n + 1, 4, i))
                if n >= 2:
                    vec.wait_ge(down_done, at(n - 1, 2, i))
                nc.vector.tensor_copy(h_hi[:, s, :], h32[:, s, :]).then_inc(h_part, 1)
                vec.wait_ge(h_part, at(2 * n + 2, 4, i))
                nc.vector.tensor_tensor(h_lo[:, s, :], h32[:, s, :], h_hi[:, s, :].bitcast(F32), ALU.subtract).then_inc(h_ready, 1)

            def finish(blk):
                vec.wait_ge(down_done, CHUNKS * (blk + 1))
                for t in range(BT):
                    step(nc.vector.bn_stats(stats[:, t, :], ps[:, t]))
                for t in range(BT):
                    nc.vector.bn_aggr(mv[:, t, :], stats[:, t, :]).then_inc(var_ready, 1)
                vec.wait_ge(std_ready, BATCH * NORMS + blk + 1)
                step(nc.vector.reciprocal(rstd[:, :], std[:, :]))
                for t in range(BT):
                    e = blk * BT + t
                    ex = 2 * BATCH * TT + e
                    if e:
                        vec.wait_ge(out_ready, e)
                    nc.vector.tensor_scalar(y[:, :], ps[:, t], mv[:, t, 0:1], rstd[:, t:t + 1], ALU.subtract, ALU.mult).then_inc(acc_out, 1)
                    vec.wait_ge(acc_out, e + 1)
                    vec.wait_ge(x_loaded[ex % 2], DMA * (ex // 2 + 1))
                    if e >= 2:
                        vec.wait_ge(out_stored[e % 2], DMA * (e // 2))
                    nc.vector.tensor_tensor(out_t[:, e % 2, :], x_in[:, ex % 2, :], y[:, :], ALU.add).then_inc(out_ready, 1)

            for blk in range(BLOCKS):
                hidden(blk * CHUNKS)
                if blk:
                    finish(blk - 1)
                hidden(blk * CHUNKS + 1)
                with vec.Fori(0, CHUNKS // 2 - 1) as i:
                    hidden(blk * CHUNKS + 2, i)
                    hidden(blk * CHUNKS + 3, i)
            finish(BLOCKS - 1)

        @block.tensor
        def _(pe):
            def three(dst, hi, lo, r_hi, r_lo, start, stop):
                nc.tensor.matmul(dst, hi, r_hi, start=start, stop=False)
                nc.tensor.matmul(dst, hi, r_lo, start=False, stop=False)
                return nc.tensor.matmul(dst, lo, r_hi, start=False, stop=stop)

            def ring(use, i=None):
                if use >= RING:
                    pe.wait_ge(bank_free, at(use - RING + 1, 2 * PER_UNIT, i))
                return ps[:, use % RING]

            def transpose_x(e, use):
                pe.wait_ge(xn_ready, e + 1)
                bank = ring(use)
                for k in range(KT):
                    last = nc.tensor.transpose(bank[:, k * P:(k + 1) * P], xn[:, e % 2, k * P:(k + 1) * P], ident[:, :])
                last.then_inc(bank_full, 1)

            def project(b, u, use, i=None):
                g = unit_no(b, u)
                s = g % 2
                pe.wait_ge(qk_split, at(g + 1, 2, i))
                for c in range(NCH):
                    bank = ring(use + c, i)
                    cols = slice(c * CH, (c + 1) * CH)
                    for k in range(KT):
                        last = three(bank, qk_hi[:, s, k, :], qk_lo[:, s, k, :], xt_hi[:, b, k, cols], xt_lo[:, b, k, cols],
                                     k == 0, k == KT - 1)
                    last.then_inc(bank_full, 1)

            def first_pass(b, u, use, n, i=None):
                s = unit_no(b, u) % 2
                h, t, half = MAXES[n]
                width = min(CH, (t + 1) * P - half * CH)
                diagonal = half * CH + width == (t + 1) * P
                bank = ring(use + n, i)
                last = nc.tensor.matmul(bank[:, 0:width], q_stack[0:QK_ROWS, s, h, t * P:(t + 1) * P],
                                        k_stack[0:QK_ROWS, s, h, half * CH:half * CH + width], start=True, stop=not diagonal)
                if diagonal:
                    last = nc.tensor.matmul(bank[:, width - P:width], ident_bf[:, :], mask_q[:, :], start=False, stop=True)
                last.then_inc(bank_full, 1)

            def stacks(b, u, i=None):
                g = unit_no(b, u)
                pe.wait_ge(stack_loaded[g % 2], at(DMA * STACK_DMAS * (g // 2 + 1), DMA * STACK_DMAS, i))

            def transpose_maxima(b, u, use, i=None):
                g = unit_no(b, u)
                pe.wait_ge(m_ready, at(g + 1, 2, i))
                for n in range(MT):
                    h, c = divmod(n, NCH)
                    bank = ring(use + n, i)
                    for t in range(CH // P):
                        last = nc.tensor.transpose(bank[0:2, t * P:(t + 1) * P], m_cols[:, h, c * CH // P + t, :].bitcast(F32), ident[:, :])
                    last.then_inc(bank_full, 1)

            def scores(b, u, j, i=None):
                g = unit_no(b, u)
                s = g % 2
                c, kt, off = STEPS[j]
                diagonal = kt * P >= c * CH
                n = 2 * (NST * g + j)
                for h in range(2):
                    if n + h >= 2:
                        pe.wait_ge(p_ready, at(n + h - 1, 4 * NST, i))
                    bank = ps[:, ST_BANK + h]
                    last = nc.tensor.matmul(bank[:, 0:CH - off], k_stack[0:ROWS, s, h, kt * P:(kt + 1) * P],
                                            q_stack[0:ROWS, s, h, c * CH + off:(c + 1) * CH], start=True, stop=not diagonal)
                    if diagonal:
                        last = nc.tensor.matmul(bank[:, 0:P], ident_bf[:, :], mask_k[:, :], start=False, stop=True)
                    last.then_inc(score_full, 1)

            def values(b, u, j, i=None):
                g = unit_no(b, u)
                s = g % 2
                c, kt, off = STEPS[j]
                if kt == 0 and NCH * g + c >= 2:
                    pe.wait_ge(acc_free, at(NCH * g + c - 1, 2 * NCH, i))
                pe.wait_ge(p_ready, at(2 * (NST * g + j) + 2, 4 * NST, i))
                for n in range(4):
                    lhs = v_pair[:, s, kt, n * HD:(n + 1) * HD] if n < 2 else ones[:, :]
                    last = nc.tensor.matmul(ps[n * HD:(n + 1) * HD, ACC_BANK + c, off:CH], lhs, probs[:, j % 2, n % 2, 0:CH - off],
                                            start=kt == 0, stop=j == CHUNK_END[c])
                last.then_inc(p_used, 1)

            def unit(b, u, use, i, ahead, projected):
                g = unit_no(b, u)
                pe.wait_ge(bank_free, at(use - NCH, 2 * PER_UNIT, i))
                pe.wait_ge(v_paired, at(g + 1, 2, i))
                scores(b, u, 0, i)
                n = 0
                for j in range(NST):
                    if j + 1 < NST:
                        scores(b, u, j + 1, i)
                    if ahead and j >= MAX_FROM:
                        if n == 0:
                            stacks(b, u + 1, i)
                        upto = NMAX * (j - MAX_FROM + 1) // (NST - MAX_FROM)
                        while n < upto:
                            first_pass(b, u + 1, use, n, i)
                            n += 1
                    values(b, u, j, i)
                if ahead:
                    transpose_maxima(b, u + 1, use + NMAX, i)
                if projected:
                    project(b, u + 2, use + NMAX + MT, i)

            pe.wait_ge(consts_made, 1)
            for b in range(BATCH):
                base = b * PER_BATCH
                for t in range(TT):
                    transpose_x(b * 2 * TT + t, base + USE_XT + t)
                pe.wait_ge(vo_split, 2 * b + 1)
                for t in range(TT):
                    pe.wait_ge(bank_free, base + USE_XT + t + 1)
                    bank = ring(base + USE_V + t)
                    cols = slice(t * P, (t + 1) * P)
                    for k in range(KT):
                        last = three(bank, xt_hi[:, b, k, cols], xt_lo[:, b, k, cols], vo_hi[:, k, :], vo_lo[:, k, :],
                                     k == 0, k == KT - 1)
                    last.then_inc(bank_full, 1)
                project(b, 0, base + USE_PROJ0)
                stacks(b, 0)
                for n in range(NMAX):
                    first_pass(b, 0, base + USE_MAX0, n)
                transpose_maxima(b, 0, base + USE_MT0)
                project(b, 1, base + USE_PROJ1)
                with pe.Fori(0, UNITS // 2 - 1) as i:
                    for s in range(2):
                        unit(b, s, base + USE_BODY + s * PER_UNIT, i, True, True)
                unit(b, UNITS - 2, base + USE_BODY + (UNITS - 2) * PER_UNIT, None, True, False)
                unit(b, UNITS - 1, base + USE_O + NCH, None, False, False)
                pe.wait_ge(vo_split, 2 * b + 2)
                pe.wait_ge(attn_split, KT * (b + 1))
                for t in range(TT + 1):
                    if t < TT:
                        bank = ring(base + use_of_o(t))
                        cols = slice(t * P, (t + 1) * P)
                        for k in range(KT):
                            last = three(bank, xt_hi[:, b, k, cols], xt_lo[:, b, k, cols], vo_hi[:, k, :], vo_lo[:, k, :],
                                         k == 0, k == KT - 1)
                        last.then_inc(bank_full, 1)
                    if t:
                        transpose_x(b * 2 * TT + TT + t - 1, base + use_of_xt2(t - 1))

            def gate_and_up(blk, n, i=None):
                s = n % 2
                b, cols = blk * BLK // SEQ, slice(blk * BLK % SEQ, blk * BLK % SEQ + BLK)
                pe.wait_ge(gu_split, at(n + 1, 2, i))
                if n >= 2:
                    pe.wait_ge(h_ready, at(n - 1, 2, i))
                for part, bank in enumerate((G_BANK, U_BANK)):
                    for k in range(KT):
                        w = slice(k * GU + part * P, k * GU + (part + 1) * P)
                        last = three(ps[:, bank + s], gu_hi[:, s, w], gu_lo[:, s, w], xt_hi[:, b, k, cols], xt_lo[:, b, k, cols], k == 0, k == KT - 1)
                    last.then_inc(gu_full, 1)

            def down(blk, n, first, final, i=None):
                s = n % 2
                pe.wait_ge(h_ready, at(n + 1, 2, i))
                pe.wait_ge(dn_split, at(n + 1, 2, i))
                for t in range(BT):
                    if first and blk:
                        pe.wait_ge(acc_out, BT * (blk - 1) + t + 1)
                    cols = slice(t * P, (t + 1) * P)
                    last = three(ps[:, t], h_hi[:, s, cols], h_lo[:, s, cols], dn_hi[:, s], dn_lo[:, s], first, final)
                last.then_inc(down_done, 1)

            pe.wait_ge(bank_free, BATCH * PER_BATCH)
            pe.wait_ge(acc_free, BATCH * UNITS * NCH)
            gate_and_up(0, 0)
            for blk in range(BLOCKS):
                n0 = blk * CHUNKS
                gate_and_up(blk, n0 + 1)
                down(blk, n0, True, False)
                with pe.Fori(0, CHUNKS // 2 - 1) as i:
                    for s in range(2):
                        gate_and_up(blk, n0 + 2 + s, i)
                        down(blk, n0 + 1 + s, False, False, i)
                if blk + 1 < BLOCKS:
                    gate_and_up(blk + 1, n0 + CHUNKS)
                down(blk, n0 + CHUNKS - 1, False, True)


def kernel(**inputs):
    import numpy as _np
    import concourse.bacc as _bacc
    from concourse import mybir as _mybir
    from concourse.bass_utils import run_bass_kernel_spmd as _run

    a = {k.removeprefix("L0_"): _np.asarray(v) for k, v in inputs.items()}
    pairs = _np.stack([a["attn_q_w"].reshape(UNITS, 2 * HD, HID), a["attn_k_w"].reshape(UNITS, 2 * HD, HID)], 1)
    bias = _np.stack([a["attn_q_b"].reshape(UNITS, 2 * HD), a["attn_k_b"].reshape(UNITS, 2 * HD)], 1).reshape(UNITS, P, 1)
    gate, up = a["ffn_w_gate_up"].reshape(2, CHUNKS, P, KT, P)
    gu = _np.stack([gate, up], 1).transpose(0, 4, 3, 1, 2).reshape(CHUNKS, P, KT * GU)
    dn = a["ffn_w_down"].reshape(HID, CHUNKS, P).transpose(1, 2, 0)
    arrays = {
        "x": a["attn_hidden_states"].reshape(BATCH * SEQ, HID),
        "qk_w": _np.concatenate([pairs.reshape(UNITS, P, KT, P).transpose(0, 3, 2, 1).reshape(UNITS, P, KT * P), bias], 2),
        "v_w": a["attn_v_w"].reshape(HID, KT, P).transpose(2, 1, 0),
        "o_w": a["attn_o_w"].reshape(HID, KT, P).transpose(2, 1, 0),
        "v_b": a["attn_v_b"],
        "o_b": a["attn_o_b"],
        "gu_w": gu,
        "dn_w": dn,
    }
    arrays = {k: _np.ascontiguousarray(v) for k, v in arrays.items()}
    nc = _bacc.Bacc("TRN2", target_bir_lowering=False, num_devices=1)
    args = [nc.dram_tensor(k, v.shape, _mybir.dt.from_np(v.dtype), kind="ExternalInput").ap() for k, v in arrays.items()]
    x1 = nc.dram_tensor("x1_dram", (BATCH * SEQ, HID), _mybir.dt.float32, kind="Internal").ap()
    out = nc.dram_tensor("out", (BATCH * SEQ, HID), _mybir.dt.float32, kind="ExternalOutput").ap()
    build(nc, *args, x1, out)
    r = _run(nc, [arrays], core_ids=[0])
    return r.results[0]["out"].reshape(BATCH, SEQ, HID)
```

```python
import concourse.bass as bass
from concourse import mybir
from contextlib import ExitStack

import numpy as np

F32 = mybir.dt.float32
F32R = mybir.dt.float32r
BF16 = mybir.dt.bfloat16
ALU = mybir.AluOpType
ACT = mybir.ActivationFunctionType
AX = mybir.AxisListType

P = 128
BATCH, SEQ, HID = 2, 1024, 512
HEADS, HD = 16, 32
INTER = 2048
KT = HID // P
TT = SEQ // P
CH = 512
NCH = SEQ // CH
UNITS = HEADS // 2
QK_ROWS = 3 * HD
ROWS = QK_ROWS + 2
SCALE = float(1.0 / np.sqrt(np.float32(HD)))
MASKED = -1.0e30
EPS = 1e-5
RING = 4
X_SLOTS = 4
FIRST_CHUNKS = (5, 6)
DMA = 16

CHUNKS = INTER // P
BLK = 512
BLOCKS = BATCH * SEQ // BLK
BT = BLK // P
GU = 2 * P

STEPS = [(c, kt, max(0, kt * P - c * CH)) for c in range(NCH) for kt in range((c + 1) * CH // P)]
NST = len(STEPS)
CHUNK_END = [max(j for j, s in enumerate(STEPS) if s[0] == c) for c in range(NCH)]
MAXES = [(h, t, 1) for h in range(2) for t in range(TT // 2)] + [(h, t, 2) for h in range(2) for t in range(TT // 2, TT)]
MAX_OFF = [sum(m[2] for m in MAXES[:n]) for n in range(len(MAXES))]
BANKS_MAX = sum(m[2] for m in MAXES)
EARLY = TT
PROJECT_STEP = max(j for j, st in enumerate(STEPS) if st[0] == 0 or st[1] < TT // 2) - 1
DONE = (2, 4, 6, 8, 8, 9, 10, 12, 14, 15, 16, 16)
BEFORE = DONE[PROJECT_STEP]
SPLIT_K = 2
STACK_DMAS = 2 * 6
ALL_UNITS = BATCH * UNITS

USE_P0 = TT
USE_V0 = USE_P0 + NCH
PER_UNIT = BANKS_MAX + NCH + 2 * NCH
OFF_PROJ = (MAX_OFF[BEFORE], PER_UNIT - 2)
AHEAD_V = 3
LAG_T = 2
MID = [("V", t) for t in range(AHEAD_V)]
END = []
for _t in range(TT + LAG_T):
    for _seq in (MID, END):
        if _t < TT:
            _seq.append(("O", _t))
        if _seq is MID and _t + AHEAD_V < TT:
            _seq.append(("V", _t + AHEAD_V))
        if _t >= LAG_T:
            _seq.append(("T", _t - LAG_T))
assert (2 * PER_UNIT) % RING == 0


def use_body(g):
    return USE_V0 + 2 * TT + (g + 1) * PER_UNIT + (len(MID) if g >= UNITS else 0) - (2 * NCH if g == ALL_UNITS - 1 else 0)


USE_MID = use_body(UNITS - 1) + PER_UNIT
USE_END = use_body(ALL_UNITS - 1)
USES = USE_END + len(END)


def use_of_xt(e):
    return e if e < TT else USE_V0 + 2 * (e - TT) + 1


def use_of(kind, b, t):
    if kind == "V" and b == 0:
        return USE_V0 + 2 * t
    if kind == "V" or b == 0:
        return USE_MID + MID.index((kind, t))
    return USE_END + END.index((kind, t))


def norm_no(b, t, second):
    n = (2 * TT - 1 if t == TT - 1 else 2 * t + 2) if second else (0 if t == 0 else 2 * t - 1)
    return BATCH * TT + b * 2 * TT + n


NORMS = 3 * BATCH * TT


def at(const, per, i):
    return const if i is None else i * per + const


def build(nc, x, qk_w, v_w, o_w, v_b, o_b, gu_w, dn_w, x1_dram, out):
    ctx = ExitStack()
    with ctx:
        def sb(stack, name, shape, dt=F32):
            return stack.enter_context(nc.sbuf_tensor(name, shape, dt))

        def sem(name):
            return ctx.enter_context(nc.semaphore(name))

        xt_hi = sb(ctx, "xt_hi", [P, BATCH, KT, SEQ], F32R)
        xt_lo = sb(ctx, "xt_lo", [P, BATCH, KT, SEQ], F32R)
        ident = sb(ctx, "ident", [P, P])
        ident_bf = sb(ctx, "ident_bf", [P, P], BF16)
        mask_q = sb(ctx, "mask_q", [P, P], BF16)
        mask_k = sb(ctx, "mask_k", [P, P], BF16)
        ones = sb(ctx, "ones", [P, HD])
        eps = sb(ctx, "eps", [P, 1])
        stats = sb(ctx, "stats", [P, BT, 6])
        mv = sb(ctx, "mv", [P, BT, 2])
        std = sb(ctx, "std", [P, BT])
        rstd = sb(ctx, "rstd", [P, BT])
        x_in = sb(ctx, "x_in", [P, X_SLOTS, HID])

        start = ExitStack()
        with start:
            vo_raw = sb(start, "vo_raw", [P, 2, KT, HID])

        att = ExitStack()
        with att:
            q_stack = sb(att, "q_stack", [P, 2, 2, SEQ], F32R)
            k_stack = sb(att, "k_stack", [P, 2, 2, SEQ], F32R)
            st_hi = sb(att, "st_hi", [P, NCH, CH], F32R)
            st_lo = sb(att, "st_lo", [P, NCH, CH], F32R)
            qk_raw = sb(att, "qk_raw", [P, 2, KT * P + 1])
            qk_hi = sb(att, "qk_hi", [P, 2, KT, P], F32R)
            qk_lo = sb(att, "qk_lo", [P, 2, KT, P], F32R)
            vw_hi = sb(att, "vw_hi", [P, KT, HID], F32R)
            vw_lo = sb(att, "vw_lo", [P, KT, HID], F32R)
            v = sb(att, "v", [P, TT, HID])
            v_pair = sb(att, "v_pair", [P, 2, TT, 2 * HD])
            attn = sb(att, "attn", [P, KT, SEQ])
            outs = sb(att, "outs", [P, CH])
            sums = sb(att, "sums", [P, CH])
            v_bias = sb(att, "v_bias", [P, HID])
            m_full = sb(att, "m_full", [P, TT, 2])
            m_cols = sb(att, "m_cols", [P, TT, P // HD, HD], F32R)
            ow_hi = sb(att, "ow_hi", [P, KT, HID], F32R)
            ow_lo = sb(att, "ow_lo", [P, KT, HID], F32R)
            xn = sb(att, "xn", [P, 2, HID])
            o_bias = sb(att, "o_bias", [P, HID])
            probs = sb(att, "probs", [P, 2, 2, CH])
        y, x1 = probs[:, 0], probs[:, 1]
        ffn = ExitStack()
        with ffn:
            gu_raw = sb(ffn, "gu_raw", [P, 2, KT * GU])
            gu_hi = sb(ffn, "gu_hi", [P, 2, KT * GU], F32R)
            gu_lo = sb(ffn, "gu_lo", [P, 2, KT * GU], F32R)
            dn_raw = sb(ffn, "dn_raw", [P, 2, HID])
            dn_hi = sb(ffn, "dn_hi", [P, 2, HID], F32R)
            dn_lo = sb(ffn, "dn_lo", [P, 2, HID], F32R)
            silu = sb(ffn, "silu", [P, 2, BLK])
            h32 = sb(ffn, "h32", [P, 2, BLK])
            h_hi = sb(ffn, "h_hi", [P, 2, BLK], F32R)
            h_lo = sb(ffn, "h_lo", [P, 2, BLK], F32R)
            acc = sb(ffn, "acc", [P, BT, HID])
            out_t = sb(ffn, "out_t", [P, 2, HID])
        ps = ctx.enter_context(nc.psum_tensor("ps", [P, 8, CH], F32))
        ps_cols = ps.rearrange("p b c -> p (b c)")
        ST_BANK, ACC_BANK = RING, RING + 2
        G_BANK, U_BANK = 4, 6

        consts_loaded = sem("consts_loaded")
        consts_made = sem("consts_made")
        x_loaded = [sem(f"x_loaded{s}") for s in range(X_SLOTS)]
        xn_ready = sem("xn_ready")
        y_ready = sem("y_ready")
        x1_ready = sem("x1_ready")
        x1_stored = [sem(f"x1_stored{s}") for s in range(2)]
        vo_loaded = [sem("vw_loaded"), sem("ow_loaded")]
        vo_split = sem("vo_split")
        qk_loaded = [sem(f"qk_loaded{s}") for s in range(2)]
        qk_split = sem("qk_split")
        pool_hi = sem("pool_hi")
        bank_full = sem("bank_full")
        bank_free = sem("bank_free")
        xt_hi_ready = sem("xt_hi_ready")
        st_hi_ready = sem("st_hi_ready")
        v_paired = sem("v_paired")
        stack_loaded = [[sem(f"stack_loaded{s}{c}") for c in range(NCH)] for s in range(2)]
        m_ready = sem("m_ready")
        m_rows0 = sem("m_rows0")
        score_full = sem("score_full")
        p_ready = sem("p_ready")
        p_used = sem("p_used")
        acc_read = sem("acc_read")
        inverted = sem("inverted")
        normalised = sem("normalised")
        attn_split = sem("attn_split")
        attn_hi_ready = sem("attn_hi_ready")
        attn_last_split = sem("attn_last_split")
        var_ready = sem("var_ready")
        std_ready = sem("std_ready")
        dve = sem("dve")
        dve_unit = sem("dve_unit")
        qk_hi_done = sem("qk_hi_done")
        gu_hi_done = sem("gu_hi_done")
        dn_hi_done = sem("dn_hi_done")
        gu_loaded = [sem(f"gu_loaded{s}") for s in range(2)]
        dn_loaded = [sem(f"dn_loaded{s}") for s in range(2)]
        gu_split = sem("gu_split")
        dn_split = sem("dn_split")
        gu_full = sem("gu_full")
        silu_ready = sem("silu_ready")
        h_part = sem("h_part")
        h_ready = sem("h_ready")
        down_done = sem("down_done")
        acc_out = sem("acc_out")
        out_ready = sem("out_ready")
        out_stored = [sem(f"out_stored{s}") for s in range(2)]

        block = ctx.enter_context(nc.Block())

        @block.sync
        def _(sp):
            sp.dma_start(v_bias[:, :], v_b.partition_broadcast(P)).then_inc(consts_loaded, DMA)
            sp.dma_start(o_bias[:, :], o_b.partition_broadcast(P)).then_inc(consts_loaded, DMA)

            def load_x(n):
                before = n - X_SLOTS
                if before >= 4 * TT:
                    sp.wait_ge(out_ready, before - 4 * TT + 1)
                elif before >= 2 * TT:
                    sp.wait_ge(x1_ready, before - 2 * TT + 1)
                elif before >= 0:
                    sp.wait_ge(xn_ready, before + 1)
                e = n % (2 * TT)
                src = x1_dram if n >= 4 * TT else x
                sp.dma_start(x_in[:, n % X_SLOTS, :], src[e * P:(e + 1) * P, :]).then_inc(x_loaded[n % X_SLOTS], DMA)

            def load_qk(g, i=None):
                if g >= 2:
                    sp.wait_ge(bank_free, at(use_body(g - 2) - PER_UNIT, 2 * PER_UNIT, i))
                u = g % UNITS
                src = qk_w[u] if i is None else qk_w[bass.ds(i * 2 + u, 1)].rearrange("a p n -> (a p) n")
                sp.dma_start(qk_raw[:, g % 2, :], src).then_inc(qk_loaded[g % 2], DMA)

            def load_stack(g, c, i=None):
                s = g % 2
                cols = slice(c * CH, (c + 1) * CH)
                for h in range(2):
                    q, k = slice(h * HD, (h + 1) * HD), slice((2 + h) * HD, (3 + h) * HD)
                    for stack, rows, part in ((q_stack, q, (st_hi, st_lo, st_hi)), (k_stack, k, (st_hi, st_hi, st_lo))):
                        for n, src in enumerate(part):
                            sp.dma_start(stack[n * HD:(n + 1) * HD, s, h, cols].bitcast(F32), src[rows, c, :].bitcast(F32)).then_inc(stack_loaded[s][c], DMA)

            def body(g, i=None):
                if 0 <= g < ALL_UNITS - 2:
                    load_qk(g + 2, i)
                if g + 1 < ALL_UNITS:
                    sp.wait_ge(bank_free, USE_V0 if g < 0 else at(use_body(g), 2 * PER_UNIT, i))
                    load_stack(g + 1, 1, i)
                if g + 2 < ALL_UNITS:
                    sp.wait_ge(bank_free, at(use_body(g) + OFF_PROJ[0] + 1, 2 * PER_UNIT, i))
                    load_stack(g + 2, 0, i)

            def residual(b, before):
                for t in range(X_SLOTS):
                    load_x((2 + b) * TT + t)
                before()
                for t in range(TT):
                    e = b * TT + t
                    sp.wait_ge(x1_ready, e + 1)
                    sp.dma_start(x1_dram[e * P:(e + 1) * P, :], x1[:, e % 2, :]).then_inc(x1_stored[e % 2], DMA)
                    if t + X_SLOTS < TT:
                        load_x((2 + b) * TT + t + X_SLOTS)

            for n in range(X_SLOTS):
                load_x(n)
                if n == 1:
                    sp.dma_start(vo_raw[:, 0], v_w).then_inc(vo_loaded[0], DMA)
                    load_qk(0)
                    load_qk(1)
            sp.dma_start(vo_raw[:, 1], o_w).then_inc(vo_loaded[1], DMA)
            for n in range(X_SLOTS, TT + X_SLOTS):
                load_x(n)
            sp.wait_ge(vo_split, 1)
            sp.wait_ge(bank_free, USE_P0 + 1)
            load_stack(0, 0)
            for n in range(TT + X_SLOTS, 2 * TT):
                load_x(n)
            sp.wait_ge(vo_split, 2)
            body(-1)
            for b in range(BATCH):
                with sp.Fori(0, UNITS // 2 - 1) as i:
                    for s in range(2):
                        body(b * UNITS + s, i)
                body(b * UNITS + UNITS - 2)
                body(b * UNITS + UNITS - 1)
                if b + 1 < BATCH:
                    residual(b, lambda: None)

            def load_w(n, c, i=None):
                s = n % 2
                gu, dn = (gu_w[c], dn_w[c]) if i is None else \
                    [w[bass.ds(i * 2 + c, 1)].rearrange("a p n -> (a p) n") for w in (gu_w, dn_w)]
                if n >= 2:
                    sp.wait_ge(gu_split, at(n - 1, 2, i))
                sp.dma_start(gu_raw[:, s], gu).then_inc(gu_loaded[s], DMA)
                if n >= 2:
                    sp.wait_ge(dn_split, at(n - 1, 2, i))
                sp.dma_start(dn_raw[:, s], dn).then_inc(dn_loaded[s], DMA)

            def first_weights():
                sp.wait_ge(p_used, NST * ALL_UNITS)
                load_w(0, 0)
                load_w(1, 1)

            residual(BATCH - 1, first_weights)
            for s in range(2):
                sp.wait_ge(x1_stored[s], DMA * BATCH * TT // 2)

            def finish(blk):
                for t in range(BT):
                    load_x(2 * BATCH * TT + blk * BT + t)
                for t in range(BT):
                    e = blk * BT + t
                    sp.wait_ge(out_ready, e + 1)
                    sp.dma_start(out[e * P:(e + 1) * P, :], out_t[:, e % 2, :]).then_inc(out_stored[e % 2], DMA)

            for blk in range(BLOCKS):
                n0 = blk * CHUNKS
                for c in range(0 if blk else 2, 4):
                    load_w(n0 + c, c)
                if blk:
                    finish(blk - 1)
                with sp.Fori(0, CHUNKS // 2 - 2) as i:
                    load_w(n0 + 4, 4, i)
                    load_w(n0 + 5, 5, i)
            finish(BLOCKS - 1)
            for s in range(2):
                sp.wait_ge(out_stored[s], DMA * BLOCKS * BT // 2)

        @block.gpsimd
        def _(pool):
            nc.gpsimd.memset(ident[:, :], 0.0).then_inc(pool_hi, 1)
            nc.gpsimd.memset(mask_q[:, :], 0.0).then_inc(pool_hi, 1)
            nc.gpsimd.memset(mask_k[:, :], 0.0).then_inc(pool_hi, 1)
            nc.gpsimd.memset(ones[:, :], 1.0).then_inc(pool_hi, 1)
            nc.gpsimd.memset(eps[:, :], EPS).then_inc(pool_hi, 1)
            nc.gpsimd.memset(m_cols[:, :, :, :].bitcast(F32), 0.0).then_inc(pool_hi, 1)
            pool.wait_ge(pool_hi, 6)
            nc.gpsimd.memset(k_stack[QK_ROWS:ROWS, :, :, :].bitcast(F32), 1.0).then_inc(pool_hi, 1)
            pool.wait_ge(pool_hi, 7)
            nc.gpsimd.affine_select(out=ident[:, :], in_=ident[:, :], compare_op=ALU.not_equal, fill=1.0,
                                    base=0, pattern=[[-1, P]], channel_multiplier=1).then_inc(pool_hi, 1)
            nc.gpsimd.affine_select(out=mask_q[:, :], in_=mask_q[:, :], compare_op=ALU.is_ge, fill=MASKED,
                                    base=0, pattern=[[-1, P]], channel_multiplier=1).then_inc(pool_hi, 1)
            nc.gpsimd.affine_select(out=mask_k[:, :], in_=mask_k[:, :], compare_op=ALU.is_ge, fill=MASKED,
                                    base=0, pattern=[[1, P]], channel_multiplier=-1).then_inc(pool_hi, 1)
            pool.wait_ge(pool_hi, 10)
            nc.gpsimd.tensor_copy(ident_bf[:, :], ident[:, :]).then_inc(consts_made, 1)
            made = [10]

            def split(hi, lo, raw, done):
                nc.gpsimd.tensor_copy(hi, raw).then_inc(pool_hi, 1)
                made[0] += 1
                pool.wait_ge(pool_hi, made[0])
                nc.gpsimd.tensor_tensor(lo, raw, hi.bitcast(F32), ALU.subtract).then_inc(done, 1)

            def qk_rest(g, i=None):
                pool.wait_ge(qk_hi_done, at(g + 1, 2, i))
                nc.gpsimd.tensor_tensor(qk_lo[:, g % 2], qk_raw[:, g % 2, 0:KT * P], qk_hi[:, g % 2].bitcast(F32),
                                        ALU.subtract).then_inc(qk_split, 1)

            def pair_values(g, i=None):
                if g >= 2:
                    pool.wait_ge(p_used, at(NST * (g - 1), 2 * NST, i))
                u = g % UNITS
                cols = bass.ds(i * (4 * HD) + u * 2 * HD, 2 * HD) if i is not None else slice(u * 2 * HD, (u + 1) * 2 * HD)
                nc.gpsimd.tensor_copy(v_pair[:, g % 2], v[:, :, cols]).then_inc(v_paired, 1)

            def gu_rest(n, i=None):
                s = n % 2
                pool.wait_ge(gu_hi_done, at(n + 1, 2, i))
                nc.gpsimd.tensor_tensor(gu_lo[:, s], gu_raw[:, s], gu_hi[:, s].bitcast(F32), ALU.subtract).then_inc(gu_split, 1)

            def dn_rest(n, i=None):
                s = n % 2
                pool.wait_ge(dn_hi_done, at(n + 1, 2, i))
                nc.gpsimd.tensor_tensor(dn_lo[:, s], dn_raw[:, s], dn_hi[:, s].bitcast(F32), ALU.subtract).then_inc(dn_split, 1)

            pool.wait_ge(vo_loaded[0], DMA)
            split(vw_hi[:, :, :], vw_lo[:, :, :], vo_raw[:, 0], vo_split)
            qk_rest(0)
            qk_rest(1)
            pool.wait_ge(vo_loaded[1], DMA)
            split(ow_hi[:, :, :], ow_lo[:, :, :], vo_raw[:, 1], vo_split)
            for b in range(BATCH):
                g0 = b * UNITS
                if b == 0:
                    pool.wait_ge(bank_free, use_of("V", b, TT - 1) + 1)
                    pair_values(g0)
                with pool.Fori(0, UNITS // 2 - 1) as i:
                    for s in range(2):
                        qk_rest(g0 + s + 2, i)
                        pair_values(g0 + s + 1, i)
                for u in (UNITS - 2, UNITS - 1):
                    if b + 1 < BATCH:
                        qk_rest(g0 + u + 2)
                    if u == UNITS - 2:
                        pair_values(g0 + UNITS - 1)
                pool.wait_ge(bank_full, use_body(g0 + UNITS - 3) + PER_UNIT)
                for k in range(KT - 1):
                    pool.wait_ge(normalised, NCH * (g0 + 2 * k + 2))
                    split(xt_hi[:, b, k, :], xt_lo[:, b, k, :], attn[:, k, :], attn_split)
                for t in range(TT):
                    e = b * TT + t
                    n = 2 * TT + e
                    pool.wait_ge(x_loaded[n % X_SLOTS], DMA * (n // X_SLOTS + 1))
                    pool.wait_ge(y_ready, e + 1)
                    if e >= 2:
                        pool.wait_ge(x1_stored[e % 2], DMA * (e // 2))
                        pool.wait_ge(xn_ready, 2 * TT + e - 1)
                    nc.gpsimd.tensor_tensor(x1[:, e % 2, :], x_in[:, n % X_SLOTS, :], y[:, e % 2, :], ALU.add).then_inc(x1_ready, 1)
                    if b + 1 < BATCH and t == TT - 2:
                        pool.wait_ge(bank_free, use_of("V", b + 1, TT - 1) + 1)
                        pair_values(g0 + UNITS)
                    if b + 1 == BATCH and t in (3, 5):
                        gu_rest(t // 2 - 1)
            dn_rest(0)
            with pool.Fori(0, BLOCKS * CHUNKS // 2 - 1) as i:
                for s in range(2):
                    gu_rest(s + 2, i)
                    dn_rest(s + 1, i)
            dn_rest(BLOCKS * CHUNKS - 1)

        @block.scalar
        def _(act):
            def root(n, slot, tiles=1):
                act.wait_ge(var_ready, n + 1 if tiles == 1 else NORMS + tiles * (n + 1 - NORMS))
                nc.scalar.activation(std[:, slot:slot + tiles], mv[:, slot:slot + tiles, 1], ACT.Sqrt, bias=eps[:, :]).then_inc(std_ready, 1)

            def hi_of_xt(b, t, use):
                act.wait_ge(bank_full, use + 1)
                nc.scalar.activation(xt_hi[:, b, :, t * P:(t + 1) * P], ps[:, use % RING].rearrange("p (k c) -> p k c", k=KT),
                                     ACT.Copy).then_inc(xt_hi_ready, 1)

            def hi_of_proj(g, c, use, i=None):
                act.wait_ge(bank_full, at(use + 1, 2 * PER_UNIT, i))
                if g >= 1:
                    act.wait_ge(stack_loaded[(g - 1) % 2][c], at(DMA * STACK_DMAS * ((g - 1) // 2 + 1), DMA * STACK_DMAS, i))
                nc.scalar.activation(st_hi[:, c, :], ps[:, use % RING], ACT.Identity, bias=qk_raw[:, g % 2, KT * P:]).then_inc(st_hi_ready, 1)

            def hi_of_qk(g, i=None):
                s = g % 2
                act.wait_ge(qk_loaded[s], at(DMA * (g // 2 + 1), DMA, i))
                nc.scalar.activation(qk_hi[:, s].rearrange("p k n -> p (k n)"), qk_raw[:, s, 0:KT * P], ACT.Copy).then_inc(qk_hi_done, 1)

            def exps(g, j, i=None):
                c, kt, off = STEPS[j]
                for h in range(2):
                    act.wait_ge(score_full, at(2 * NST * g + 2 * j + h + 1, 4 * NST, i))
                    if g * NST + j >= 2 and h == 0:
                        act.wait_ge(p_used, at(NST * g + j - 1, 2 * NST, i))
                    nc.scalar.activation(probs[:, j % 2, h, 0:CH - off], ps[:, ST_BANK + h, 0:CH - off], ACT.Exp,
                                         scale=SCALE).then_inc(p_ready, 1)

            def copy_acc(g, c, i=None):
                act.wait_ge(p_used, at(NST * g + CHUNK_END[c] + 1, 2 * NST, i))
                if g and c == 0:
                    act.wait_ge(normalised, at(NCH * g, 2 * NCH, i))
                rows = slice(c * 2 * HD, (c + 1) * 2 * HD)
                nc.scalar.activation(outs[rows, :], ps[0:2 * HD, ACC_BANK + c], ACT.Copy).then_inc(acc_read, 1)
                nc.scalar.activation(sums[rows, :], ps[2 * HD:4 * HD, ACC_BANK + c], ACT.Copy).then_inc(acc_read, 1)

            def hi_of_attn(b, c):
                g = (b + 1) * UNITS - 1
                act.wait_ge(bank_full, use_body(g - 2) + PER_UNIT)
                act.wait_ge(normalised, NCH * g + c + 1)
                cols = slice(c * CH, (c + 1) * CH)
                nc.scalar.activation(xt_hi[:, b, KT - 1, cols], attn[:, KT - 1, cols], ACT.Copy).then_inc(attn_hi_ready, 1)

            def max_rows(g, use, i=None):
                for c in range(NCH):
                    act.wait_ge(bank_full, at(use + c + 1, 2 * PER_UNIT, i))
                    nc.scalar.activation(q_stack[QK_ROWS:ROWS, g % 2, 0, c * CH:(c + 1) * CH], ps[0:2, (use + c) % RING], ACT.Copy).then_inc(m_rows0, 1)

            def body(g, i=None):
                use = use_body(g)
                projected = g + 2 < ALL_UNITS
                for j in range(NST if g >= 0 else 0):
                    exps(g, j, i)
                    if projected and j == 1:
                        hi_of_qk(g + 2, i)
                    if projected and j == PROJECT_STEP + 1:
                        hi_of_proj(g + 2, 0, use + OFF_PROJ[0], i)
                    if g == ALL_UNITS - 1 and j == PROJECT_STEP:
                        copy_acc(g, 0, i)
                    if g == ALL_UNITS - 1 and j == NST - 2:
                        hi_of_attn(g // UNITS, 0)
                if projected and g < 0:
                    hi_of_proj(g + 2, 0, use + OFF_PROJ[0], i)
                if 0 <= g < ALL_UNITS - 1:
                    copy_acc(g, 0, i)
                if g >= 0:
                    copy_acc(g, 1, i)
                if g + 1 < ALL_UNITS:
                    max_rows(g + 1, use + BANKS_MAX + (2 if projected else 0), i)
                if projected:
                    hi_of_proj(g + 2, 1, use + OFF_PROJ[1], i)

            def residual(b, extra):
                for t in range(TT + LAG_T):
                    if t < TT:
                        root(norm_no(b, t, False), 0)
                    if 1 <= t <= TT:
                        root(norm_no(b, t - 1, True), 1)
                    if t >= LAG_T:
                        hi_of_xt(b, t - LAG_T, use_of("T", b, t - LAG_T))
                    extra(t)

            act.wait_ge(consts_loaded, 2 * DMA)
            act.wait_ge(consts_made, 1)
            for e in range(2 * TT + 2):
                if e < 2 * TT:
                    root(e, e % 2)
                if e >= 2:
                    hi_of_xt((e - 2) // TT, (e - 2) % TT, use_of_xt(e - 2))
                if e == 3:
                    hi_of_qk(0)
                    hi_of_qk(1)
                if e - 2 == TT - 1:
                    for c in range(NCH):
                        hi_of_proj(0, c, USE_P0 + c)
            body(-1)

            def silus(n, i=None):
                s = n % 2
                act.wait_ge(gu_full, at(2 * n + 1, 4, i))
                if n >= 2:
                    act.wait_ge(h_ready, at(n - 1, 2, i))
                nc.scalar.activation(silu[:, s, :], ps[:, G_BANK + s], ACT.Silu).then_inc(silu_ready, 1)

            def hi_of_gu(n, i=None):
                s = n % 2
                act.wait_ge(gu_loaded[s], at(DMA * (n // 2 + 1), DMA, i))
                if n >= 2:
                    act.wait_ge(gu_full, at(2 * n - 2, 4, i))
                nc.scalar.activation(gu_hi[:, s], gu_raw[:, s], ACT.Copy).then_inc(gu_hi_done, 1)

            def hi_of_dn(n, i=None):
                s = n % 2
                act.wait_ge(dn_loaded[s], at(DMA * (n // 2 + 1), DMA, i))
                if n >= 2:
                    act.wait_ge(down_done, at(n - 1, 2, i))
                nc.scalar.activation(dn_hi[:, s], dn_raw[:, s], ACT.Copy).then_inc(dn_hi_done, 1)

            def first_weights(t):
                if t in (2, 4):
                    hi_of_gu(t // 2 - 1)
                elif t == 5:
                    hi_of_dn(0)

            for b in range(BATCH):
                g0 = b * UNITS
                for s in range(2) if b else ():
                    act.wait_ge(x1_stored[s], DMA * b * TT // 2)
                with act.Fori(0, UNITS // 2 - 1) as i:
                    for s in range(2):
                        body(g0 + s, i)
                body(g0 + UNITS - 2)
                body(g0 + UNITS - 1)
                for c in range(NCH - 1 if b + 1 == BATCH else 0, NCH):
                    hi_of_attn(b, c)
                residual(b, first_weights if b + 1 == BATCH else lambda t: None)

            def chunk(n, i=None):
                silus(n, i)
                if n < BLOCKS * CHUNKS - 2:
                    hi_of_gu(n + 2, i)
                if n < BLOCKS * CHUNKS - 1:
                    hi_of_dn(n + 1, i)

            for blk in range(BLOCKS):
                n0 = blk * CHUNKS
                chunk(n0)
                if blk:
                    root(NORMS + blk - 1, 0, BT)
                chunk(n0 + 1)
                with act.Fori(0, CHUNKS // 2 - 2) as i:
                    chunk(n0 + 2, i)
                    chunk(n0 + 3, i)
                chunk(n0 + CHUNKS - 2)
                chunk(n0 + CHUNKS - 1)
            root(NORMS + BLOCKS - 1, 0, BT)

        @block.vector
        def _(vec):
            n_dve = [0]

            def step(ins):
                n_dve[0] += 1
                ins.then_inc(dve, 1)
                vec.wait_ge(dve, n_dve[0])

            def moments(src, slot):
                step(nc.vector.bn_stats(stats[:, slot, :], src))
                nc.vector.bn_aggr(mv[:, slot, :], stats[:, slot, :]).then_inc(var_ready, 1)

            def normed(dst, src, n, slot):
                vec.wait_ge(std_ready, n + 1)
                step(nc.vector.reciprocal(rstd[:, slot:slot + 1], std[:, slot:slot + 1]))
                return nc.vector.tensor_scalar(dst, src, mv[:, slot, 0:1], rstd[:, slot:slot + 1], ALU.subtract, ALU.mult)

            tiles_lo = [0]

            def lo_of_xt(b, t, use):
                tiles_lo[0] += 1
                vec.wait_ge(xt_hi_ready, tiles_lo[0])
                cols = slice(t * P, (t + 1) * P)
                nc.vector.tensor_tensor(xt_lo[:, b, :, cols], ps[:, use % RING].rearrange("p (k c) -> p k c", k=KT),
                                        xt_hi[:, b, :, cols].bitcast(F32), ALU.subtract).then_inc(bank_free, 1)

            def lo_of_proj(g, c, use, i=None, banks=2):
                vec.wait_ge(st_hi_ready, at(NCH * g + c + 1, 2 * NCH, i))
                nc.vector.scalar_tensor_tensor(st_lo[:, c, :], ps[:, use % RING], qk_raw[:, g % 2, KT * P:], st_hi[:, c, :].bitcast(F32),
                                               ALU.add, ALU.subtract).then_inc(bank_free, banks)

            def values(b, t):
                use = use_of("V", b, t)
                vec.wait_ge(bank_full, use + 1)
                if b and t == 0:
                    vec.wait_ge(v_paired, b * UNITS)
                nc.vector.tensor_tensor(v[:, t, :], ps[:, use % RING], v_bias[:, :], ALU.add).then_inc(bank_free, 1)

            def maxima(tiles, use, i=None):
                for n in tiles:
                    h, t, banks = MAXES[n]
                    first = use + MAX_OFF[n]
                    vec.wait_ge(bank_full, at(first + banks, 2 * PER_UNIT, i))
                    scores = ps_cols[:, first % RING * CH:first % RING * CH + (t + 1) * P]
                    nc.vector.reduce_max(m_full[:, t, h:h + 1], scores, AX.X).then_inc(bank_free, banks)

            def negated(g, use, i=None):
                vec.wait_ge(bank_free, at(use, 2 * PER_UNIT, i))
                nc.vector.tensor_scalar(m_cols[:, :, 0:2, 0], m_full[:, :, :], -1.0, None, ALU.mult).then_inc(dve_unit, 1)
                vec.wait_ge(dve_unit, at(g + 1, 2, i))
                nc.vector.scalar_tensor_tensor(m_cols[:, :, 0:2, 1], m_full[:, :, :], -1.0, m_cols[:, :, 0:2, 0].bitcast(F32),
                                               ALU.mult, ALU.subtract).then_inc(m_ready, 1)

            def max_rows(g, use, i=None):
                for c in range(NCH):
                    vec.wait_ge(bank_full, at(use + c + 1, 2 * PER_UNIT, i))
                    vec.wait_ge(m_rows0, at(NCH * g + c + 1, 2 * NCH, i))
                    nc.vector.tensor_copy(q_stack[QK_ROWS:ROWS, g % 2, 1, c * CH:(c + 1) * CH], ps[HD:HD + 2, (use + c) % RING]).then_inc(bank_free, 1)

            def normalise(g, i=None):
                vec.wait_ge(acc_read, at(2 * NCH * (g + 1), 4 * NCH, i))
                nc.vector.reciprocal(sums[:, :], sums[:, :]).then_inc(inverted, 1)
                vec.wait_ge(inverted, at(g + 1, 2, i))
                rows = slice((g % 2) * 2 * HD, (g % 2 + 1) * 2 * HD)
                k = g % UNITS // 2
                for c in range(NCH):
                    part = slice(c * 2 * HD, (c + 1) * 2 * HD)
                    dst = attn[rows, k, c * CH:(c + 1) * CH] if i is None else \
                        attn[rows, bass.ds(i + k, 1), c * CH:(c + 1) * CH].rearrange("p a c -> p (a c)")
                    nc.vector.tensor_tensor(dst, outs[part, :], sums[part, :], ALU.mult).then_inc(normalised, 1)

            def normalise_last(g, c):
                vec.wait_ge(acc_read, 2 * (NCH * g + c + 1))
                part, cols = slice(c * 2 * HD, (c + 1) * 2 * HD), slice(c * CH, (c + 1) * CH)
                step(nc.vector.reciprocal(sums[part, :], sums[part, :]))
                nc.vector.tensor_tensor(attn[(g % 2) * 2 * HD:(g % 2 + 1) * 2 * HD, KT - 1, cols], outs[part, :], sums[part, :], ALU.mult).then_inc(normalised, 1)

            def lo_of_attn(b, c):
                vec.wait_ge(attn_hi_ready, NCH * b + c + 1)
                cols = slice(c * CH, (c + 1) * CH)
                nc.vector.tensor_tensor(xt_lo[:, b, KT - 1, cols], attn[:, KT - 1, cols], xt_hi[:, b, KT - 1, cols].bitcast(F32),
                                        ALU.subtract).then_inc(attn_last_split, 1)

            def body(g, i=None):
                use = use_body(g)
                projected = g + 2 < ALL_UNITS
                if g + 1 < ALL_UNITS:
                    maxima(range(BEFORE), use, i)
                    if projected:
                        lo_of_proj(g + 2, 0, use + OFF_PROJ[0], i)
                    late = use + (2 if projected else 0)
                    maxima(range(BEFORE, len(MAXES)), late, i)
                    negated(g + 1, late + BANKS_MAX, i)
                    max_rows(g + 1, late + BANKS_MAX, i)
                if projected:
                    lo_of_proj(g + 2, 1, use + OFF_PROJ[1], i)
                if 0 <= g < ALL_UNITS - 1:
                    normalise(g, i)

            def residual(b):
                for t in range(AHEAD_V if b + 1 < BATCH else 0):
                    values(b + 1, t)
                for t in range(TT + LAG_T):
                    if t < TT:
                        use, e = use_of("O", b, t), b * TT + t
                        vec.wait_ge(bank_full, use + 1)
                        nc.vector.tensor_tensor(y[:, e % 2, :], ps[:, use % RING], o_bias[:, :], ALU.add).then_inc(bank_free, 1)
                        if b + 1 < BATCH and t + AHEAD_V < TT:
                            values(b + 1, t + AHEAD_V)
                        vec.wait_ge(bank_free, use + 1)
                        moments(y[:, e % 2, :], 0)
                    if 1 <= t <= TT:
                        e1 = b * TT + t - 1
                        vec.wait_ge(x1_ready, e1 + 1)
                        moments(x1[:, e1 % 2, :], 1)
                    if t < TT:
                        normed(y[:, e % 2, :], y[:, e % 2, :], norm_no(b, t, False), 0).then_inc(y_ready, 1)
                    if 1 <= t <= TT:
                        normed(xn[:, e1 % 2, :], x1[:, e1 % 2, :], norm_no(b, t - 1, True), 1).then_inc(xn_ready, 1)
                    if t >= LAG_T:
                        lo_of_xt(b, t - LAG_T, use_of("T", b, t - LAG_T))

            vec.wait_ge(consts_loaded, 2 * DMA)
            for e in range(2 * TT + 2):
                if e < 2 * TT:
                    vec.wait_ge(x_loaded[e % X_SLOTS], DMA * (e // X_SLOTS + 1))
                    moments(x_in[:, e % X_SLOTS, :], e % 2)
                if 1 <= e <= 2 * TT:
                    d = e - 1
                    normed(xn[:, d % 2, :], x_in[:, d % X_SLOTS, :], d, d % 2).then_inc(xn_ready, 1)
                if e >= 2:
                    d = e - 2
                    if d >= TT:
                        values(0, d - TT)
                    lo_of_xt(d // TT, d % TT, use_of_xt(d))
                    if d == TT - 1:
                        for c in range(NCH):
                            lo_of_proj(0, c, USE_P0 + c, banks=1)
            body(-1)
            for b in range(BATCH):
                g0 = b * UNITS
                if b:
                    vec.wait_ge(attn_split, (KT - 1) * b)
                with vec.Fori(0, UNITS // 2 - 1) as i:
                    for s in range(2):
                        body(g0 + s, i)
                body(g0 + UNITS - 2)
                body(g0 + UNITS - 1)
                for c in range(NCH):
                    if b + 1 == BATCH:
                        normalise_last(g0 + UNITS - 1, c)
                    lo_of_attn(b, c)
                residual(b)

            def hidden(n, i=None):
                s = n % 2
                vec.wait_ge(silu_ready, at(n + 1, 2, i))
                vec.wait_ge(gu_full, at(2 * n + 2, 4, i))
                nc.vector.tensor_tensor(h32[:, s, :], ps[:, U_BANK + s], silu[:, s, :], ALU.mult).then_inc(h_part, 1)
                vec.wait_ge(h_part, at(2 * n + 1, 4, i))
                if n >= 2:
                    vec.wait_ge(down_done, at(n - 1, 2, i))
                nc.vector.tensor_copy(h_hi[:, s, :], h32[:, s, :]).then_inc(h_part, 1)
                vec.wait_ge(h_part, at(2 * n + 2, 4, i))
                nc.vector.tensor_tensor(h_lo[:, s, :], h32[:, s, :], h_hi[:, s, :].bitcast(F32), ALU.subtract).then_inc(h_ready, 1)

            def finish(blk):
                vec.wait_ge(down_done, CHUNKS * (blk + 1))
                for t in range(BT):
                    nc.vector.tensor_copy(acc[:, t, :], ps[:, t]).then_inc(acc_out, 1)
                vec.wait_ge(acc_out, BT * (blk + 1))
                for t in range(BT):
                    step(nc.vector.bn_stats(stats[:, t, :], acc[:, t, :]))
                for t in range(BT):
                    nc.vector.bn_aggr(mv[:, t, :], stats[:, t, :]).then_inc(var_ready, 1)
                vec.wait_ge(std_ready, NORMS + blk + 1)
                step(nc.vector.reciprocal(rstd[:, :], std[:, :]))
                for t in range(BT):
                    e = blk * BT + t
                    ex = 2 * BATCH * TT + e
                    step(nc.vector.tensor_scalar(acc[:, t, :], acc[:, t, :], mv[:, t, 0:1], rstd[:, t:t + 1], ALU.subtract, ALU.mult))
                    vec.wait_ge(x_loaded[ex % X_SLOTS], DMA * (ex // X_SLOTS + 1))
                    if e >= 2:
                        vec.wait_ge(out_stored[e % 2], DMA * (e // 2))
                    nc.vector.tensor_tensor(out_t[:, e % 2, :], x_in[:, ex % X_SLOTS, :], acc[:, t, :], ALU.add).then_inc(out_ready, 1)

            for blk in range(BLOCKS):
                hidden(blk * CHUNKS)
                if blk:
                    finish(blk - 1)
                hidden(blk * CHUNKS + 1)
                with vec.Fori(0, CHUNKS // 2 - 1) as i:
                    hidden(blk * CHUNKS + 2, i)
                    hidden(blk * CHUNKS + 3, i)
            finish(BLOCKS - 1)

        @block.tensor
        def _(pe):
            def three(dst, hi, lo, r_hi, r_lo, start, stop):
                nc.tensor.matmul(dst, hi, r_hi, start=start, stop=False)
                nc.tensor.matmul(dst, hi, r_lo, start=False, stop=False)
                return nc.tensor.matmul(dst, lo, r_hi, start=False, stop=stop)

            def ring(use, i=None):
                if use >= RING:
                    pe.wait_ge(bank_free, at(use - RING + 1, 2 * PER_UNIT, i))
                return ps[:, use % RING]

            def transpose_x(n, use):
                pe.wait_ge(xn_ready, n + 1)
                bank = ring(use)
                for k in range(KT):
                    last = nc.tensor.transpose(bank[:, k * P:(k + 1) * P], xn[:, n % 2, k * P:(k + 1) * P], ident[:, :])
                last.then_inc(bank_full, 1)

            def tokens_by_weights(b, t, hi, lo, use):
                bank = ring(use)
                cols = slice(t * P, (t + 1) * P)
                for k in range(KT):
                    last = three(bank, xt_hi[:, b, k, cols], xt_lo[:, b, k, cols], hi[:, k, :], lo[:, k, :], k == 0, k == KT - 1)
                last.then_inc(bank_full, 1)

            def project(g, b, c, use, i=None, ks=range(KT), banks=2):
                s = g % 2
                if c == 0:
                    pe.wait_ge(qk_split, at(g + 1, 2, i))
                bank = ring(use, i) if ks[0] == 0 else ps[:, use % RING]
                cols = slice(c * CH, (c + 1) * CH)
                for k in ks:
                    last = three(bank, qk_hi[:, s, k, :], qk_lo[:, s, k, :], xt_hi[:, b, k, cols], xt_lo[:, b, k, cols],
                                 k == 0, k == KT - 1)
                if ks[-1] == KT - 1:
                    last.then_inc(bank_full, banks)

            def first_pass(g, n, use, i=None):
                s = g % 2
                if n in (0, EARLY):
                    pe.wait_ge(stack_loaded[s][0 if n == 0 else 1], at(DMA * STACK_DMAS * (g // 2 + 1), DMA * STACK_DMAS, i))
                h, t, banks = MAXES[n]
                ring(use + banks - 1, i)
                for half in range(banks):
                    bank = ps[:, (use + half) % RING]
                    width = min(CH, (t + 1) * P - half * CH)
                    diagonal = half == banks - 1
                    last = nc.tensor.matmul(bank[:, 0:width], q_stack[0:QK_ROWS, s, h, t * P:(t + 1) * P],
                                            k_stack[0:QK_ROWS, s, h, half * CH:half * CH + width], start=True, stop=not diagonal)
                    if diagonal:
                        last = nc.tensor.matmul(bank[:, width - P:width], ident_bf[:, :], mask_q[:, :], start=False, stop=True)
                last.then_inc(bank_full, banks)

            def transpose_maxima(g, use, i=None):
                pe.wait_ge(m_ready, at(g + 1, 2, i))
                for c in range(NCH):
                    bank = ring(use + c, i)
                    for t in range(CH // P):
                        cols = m_cols[:, c * CH // P + t].rearrange("p h n -> p (h n)").bitcast(F32)
                        last = nc.tensor.transpose(bank[:, t * P:(t + 1) * P], cols, ident[:, :])
                    last.then_inc(bank_full, 1)

            def scores(g, j, i=None):
                s = g % 2
                c, kt, off = STEPS[j]
                if kt == 0:
                    pe.wait_ge(bank_free, at(use_body(g) - NCH - (0 if g == ALL_UNITS - 1 else 2) + c + 1, 2 * PER_UNIT, i))
                diagonal = kt * P >= c * CH
                n = 2 * (NST * g + j)
                for h in range(2):
                    if n + h >= 2:
                        pe.wait_ge(p_ready, at(n + h - 1, 4 * NST, i))
                    bank = ps[:, ST_BANK + h]
                    last = nc.tensor.matmul(bank[:, 0:CH - off], k_stack[0:ROWS, s, h, kt * P:(kt + 1) * P],
                                            q_stack[0:ROWS, s, h, c * CH + off:(c + 1) * CH], start=True, stop=not diagonal)
                    if diagonal:
                        last = nc.tensor.matmul(bank[:, 0:P], ident_bf[:, :], mask_k[:, :], start=False, stop=True)
                    last.then_inc(score_full, 1)

            def values(g, j, i=None):
                s = g % 2
                c, kt, off = STEPS[j]
                if kt == 0 and g >= 1:
                    pe.wait_ge(acc_read, at(2 * (NCH * (g - 1) + c + 1), 4 * NCH, i))
                pe.wait_ge(p_ready, at(2 * (NST * g + j) + 2, 4 * NST, i))
                for n in range(4):
                    lhs = v_pair[:, s, kt, n * HD:(n + 1) * HD] if n < 2 else ones[:, :]
                    last = nc.tensor.matmul(ps[n * HD:(n + 1) * HD, ACC_BANK + c, off:CH], lhs, probs[:, j % 2, n % 2, 0:CH - off],
                                            start=kt == 0, stop=j == CHUNK_END[c])
                last.then_inc(p_used, 1)

            def body(g, i=None):
                use = use_body(g)
                ahead, projected = g + 1 < ALL_UNITS, g + 2 < ALL_UNITS
                batch = (g + 2) // UNITS
                if g >= 0:
                    pe.wait_ge(v_paired, at(g + 1, 2, i))
                    scores(g, 0, i)
                late = 0
                n = 0
                for j in range(NST):
                    if g >= 0 and 0 < j < NST - 1:
                        scores(g, j + 1, i)
                    while ahead and n < DONE[j]:
                        first_pass(g + 1, n, use + late + MAX_OFF[n], i)
                        n += 1
                    if projected and j == PROJECT_STEP:
                        project(g + 2, batch, 0, use + OFF_PROJ[0], i)
                        late = 2
                    if g >= 0 and j == 0:
                        scores(g, 1, i)
                    if g >= 0:
                        values(g, j, i)
                if projected:
                    project(g + 2, batch, 1, use + OFF_PROJ[1], i, range(0, SPLIT_K))
                if ahead:
                    transpose_maxima(g + 1, use + late + BANKS_MAX, i)
                if projected:
                    project(g + 2, batch, 1, use + OFF_PROJ[1], i, range(SPLIT_K, KT))

            def residual(b, order, extra):
                for n, (kind, t) in enumerate(order):
                    if kind == "V":
                        tokens_by_weights(b + 1, t, vw_hi, vw_lo, use_of("V", b + 1, t))
                    elif kind == "O":
                        if t == 0:
                            pe.wait_ge(attn_split, (KT - 1) * (b + 1))
                        if t % (TT // NCH) == 0:
                            pe.wait_ge(attn_last_split, NCH * b + t // (TT // NCH) + 1)
                        tokens_by_weights(b, t, ow_hi, ow_lo, use_of("O", b, t))
                    else:
                        transpose_x(2 * TT + b * TT + t, use_of("T", b, t))
                    extra(kind, t)

            def gate_and_up(blk, n, i=None):
                s = n % 2
                b, cols = blk * BLK // SEQ, slice(blk * BLK % SEQ, blk * BLK % SEQ + BLK)
                pe.wait_ge(gu_split, at(n + 1, 2, i))
                if n >= 2:
                    pe.wait_ge(h_ready, at(n - 1, 2, i))
                for part, bank in enumerate((G_BANK, U_BANK)):
                    for k in range(KT):
                        w = slice(k * GU + part * P, k * GU + (part + 1) * P)
                        last = three(ps[:, bank + s], gu_hi[:, s, w], gu_lo[:, s, w], xt_hi[:, b, k, cols], xt_lo[:, b, k, cols], k == 0, k == KT - 1)
                    last.then_inc(gu_full, 1)

            def down(blk, n, first, final, i=None):
                s = n % 2
                pe.wait_ge(h_ready, at(n + 1, 2, i))
                pe.wait_ge(dn_split, at(n + 1, 2, i))
                for t in range(BT):
                    if first and blk:
                        pe.wait_ge(acc_out, BT * (blk - 1) + t + 1)
                    cols = slice(t * P, (t + 1) * P)
                    last = three(ps[:, t], h_hi[:, s, cols], h_lo[:, s, cols], dn_hi[:, s], dn_lo[:, s], first, final)
                last.then_inc(down_done, 1)

            def first_chunks(kind, t):
                if kind == "T" and t in FIRST_CHUNKS:
                    if t == FIRST_CHUNKS[0]:
                        pe.wait_ge(acc_read, 2 * NCH * ALL_UNITS)
                    gate_and_up(0, FIRST_CHUNKS.index(t))

            pe.wait_ge(consts_made, 1)
            for t in range(TT):
                transpose_x(t, use_of_xt(t))
            pe.wait_ge(bank_free, TT)
            for c in range(NCH):
                project(0, 0, c, USE_P0 + c, banks=1)
            pe.wait_ge(vo_split, 1)
            for t in range(TT):
                tokens_by_weights(0, t, vw_hi, vw_lo, use_of("V", 0, t))
                transpose_x(TT + t, use_of_xt(TT + t))
            body(-1)
            pe.wait_ge(vo_split, 2)
            for b in range(BATCH):
                g0 = b * UNITS
                with pe.Fori(0, UNITS // 2 - 1) as i:
                    for s in range(2):
                        body(g0 + s, i)
                body(g0 + UNITS - 2)
                body(g0 + UNITS - 1)
                if b + 1 < BATCH:
                    residual(b, MID, lambda kind, t: None)
                else:
                    residual(b, END, first_chunks)

            pe.wait_ge(bank_free, USES)
            for blk in range(BLOCKS):
                n0 = blk * CHUNKS
                if blk:
                    gate_and_up(blk, n0 + 1)
                down(blk, n0, True, False)
                with pe.Fori(0, CHUNKS // 2 - 1) as i:
                    for s in range(2):
                        gate_and_up(blk, n0 + 2 + s, i)
                        down(blk, n0 + 1 + s, False, False, i)
                if blk + 1 < BLOCKS:
                    gate_and_up(blk + 1, n0 + CHUNKS)
                down(blk, n0 + CHUNKS - 1, False, True)


def kernel(**inputs):
    import numpy as _np
    import concourse.bacc as _bacc
    from concourse import mybir as _mybir
    from concourse.bass_utils import run_bass_kernel_spmd as _run

    a = {k.removeprefix("L0_"): _np.asarray(v) for k, v in inputs.items()}
    pairs = _np.stack([a["attn_q_w"].reshape(UNITS, 2 * HD, HID), a["attn_k_w"].reshape(UNITS, 2 * HD, HID)], 1)
    bias = _np.stack([a["attn_q_b"].reshape(UNITS, 2 * HD), a["attn_k_b"].reshape(UNITS, 2 * HD)], 1).reshape(UNITS, P, 1)
    gate, up = a["ffn_w_gate_up"].reshape(2, CHUNKS, P, KT, P)
    gu = _np.stack([gate, up], 1).transpose(0, 4, 3, 1, 2).reshape(CHUNKS, P, KT * GU)
    dn = a["ffn_w_down"].reshape(HID, CHUNKS, P).transpose(1, 2, 0)
    arrays = {
        "x": a["attn_hidden_states"].reshape(BATCH * SEQ, HID),
        "qk_w": _np.concatenate([pairs.reshape(UNITS, P, KT, P).transpose(0, 3, 2, 1).reshape(UNITS, P, KT * P), bias], 2),
        "v_w": a["attn_v_w"].reshape(HID, KT, P).transpose(2, 1, 0),
        "o_w": a["attn_o_w"].reshape(HID, KT, P).transpose(2, 1, 0),
        "v_b": a["attn_v_b"],
        "o_b": a["attn_o_b"],
        "gu_w": gu,
        "dn_w": dn,
    }
    arrays = {k: _np.ascontiguousarray(v) for k, v in arrays.items()}
    nc = _bacc.Bacc("TRN2", target_bir_lowering=False, num_devices=1, dynamic_dma_scratch_size=1024)
    args = [nc.dram_tensor(k, v.shape, _mybir.dt.from_np(v.dtype), kind="ExternalInput").ap() for k, v in arrays.items()]
    x1 = nc.dram_tensor("x1_dram", (BATCH * SEQ, HID), _mybir.dt.float32, kind="Internal").ap()
    out = nc.dram_tensor("out", (BATCH * SEQ, HID), _mybir.dt.float32, kind="ExternalOutput").ap()
    build(nc, *args, x1, out)
    r = _run(nc, [arrays], core_ids=[0])
    return r.results[0]["out"].reshape(BATCH, SEQ, HID)
```

```python
import concourse.bass as bass
from concourse import mybir
from contextlib import ExitStack

import numpy as np

F32 = mybir.dt.float32
F32R = mybir.dt.float32r
BF16 = mybir.dt.bfloat16
ALU = mybir.AluOpType
ACT = mybir.ActivationFunctionType

P = 128
BATCH, SEQ, HID = 2, 1024, 512
HEADS, HD = 16, 32
INTER = 2048
KT = HID // P
TT = SEQ // P
CH = 512
NCH = SEQ // CH
UNITS = HEADS // 2
QK_ROWS = 3 * HD
ROWS = QK_ROWS + 2
SCALE = float(1.0 / np.sqrt(np.float32(HD)))
MASKED = -1.0e30
EPS = 1e-5
RING = 4
X_SLOTS = 5
DMA = 16

CHUNKS = INTER // P
BLK = 512
BLOCKS = BATCH * SEQ // BLK
BT = BLK // P
GU = 2 * P

STEPS = [(c, kt, max(0, kt * P - c * CH)) for c in range(NCH) for kt in range((c + 1) * CH // P)]
NST = len(STEPS)
CHUNK_END = [max(j for j, s in enumerate(STEPS) if s[0] == c) for c in range(NCH)]
MAXES = [(h, t, 1) for h in range(2) for t in range(TT // 2)] + [(h, t, 2) for h in range(2) for t in range(TT // 2, TT)]
MAX_OFF = [sum(m[2] for m in MAXES[:n]) for n in range(len(MAXES))]
BANKS_MAX = sum(m[2] for m in MAXES)
EARLY = TT
PROJECT_STEP = 6
STAGE_STEP = max(j for j, st in enumerate(STEPS) if st[0] == 0 or st[1] < TT // 2)
DONE = (4, 5, 6, 8, 8, 8, 9, 11, 13, 15, 16, 16)
BEFORE = DONE[PROJECT_STEP]
COPY_STEP = 8
AT_NORM = 4
SPLIT_K = 2
STACK_DMAS = 2 * 6
ALL_UNITS = BATCH * UNITS

LAG_X = 2
AHEAD_X = 6
PROJECT_AFTER = {TT - 1: ((0, 0),), TT: ((0, 1),), 2 * TT - 3: ((1, 0),)}
START, _v = [], 0
for _t in range(2 * TT):
    START.append(("X", _t))
    for _p in PROJECT_AFTER.get(_t, ()):
        START.append(("P", _p))
        START += [("pad", _p)] * _p[0]
    if _t >= AHEAD_X - 1 and _t not in PROJECT_AFTER and _v < TT:
        START.append(("V", _v))
        _v += 1
assert _v == TT
PER_UNIT = BANKS_MAX + 2 + NCH
OFF_PROJ = MAX_OFF[BEFORE]
V_STEPS = (-1, -1, 0, 2, 4, 6, 8, 9)
LAG_T = (3, 3)
FIRST_CHUNKS = (("O", 3), ("T", 5))
MID = [("V", t) for t, _s in enumerate(V_STEPS) if _s < 0]
END = []
for _seq, _lag in ((MID, LAG_T[0]), (END, LAG_T[1])):
    for _t in range(TT + _lag):
        if _t < TT:
            _seq.append(("O", _t))
        if _t >= _lag:
            _seq.append(("T", _t - _lag))
        if _seq is MID and _t in V_STEPS:
            _seq.append(("V", V_STEPS.index(_t)))
assert (2 * PER_UNIT) % RING == 0


def use_body(g):
    start = len(START) + (PER_UNIT - 2 if g >= 0 else 0)
    return start + max(g, 0) * PER_UNIT + (len(MID) if g >= UNITS else 0) - (2 if g == ALL_UNITS - 1 else 0)


USE_MID = use_body(UNITS - 1) + PER_UNIT
USE_END = use_body(ALL_UNITS - 1)
USES = USE_END + len(END)


def use_max_rows(g):
    return use_body(g) + BANKS_MAX + (2 if 0 <= g < ALL_UNITS - 2 else 0)


def use_of_p(g, c):
    return START.index(("P", (g, c)))


def use_of_xt(e):
    return START.index(("X", e))


def use_of(kind, b, t):
    if kind == "V" and b == 0:
        return START.index(("V", t))
    if kind == "V" or b == 0:
        return USE_MID + MID.index((kind, t))
    return USE_END + END.index((kind, t))


NORMS = 3 * BATCH * TT
ROOTS = 2 * TT + BATCH * (TT + 1)


def at(const, per, i):
    return const if i is None else i * per + const


def build(nc, x, qk_w, v_w, o_w, v_b, o_b, gu_w, dn_w, x1_dram, out):
    ctx = ExitStack()
    with ctx:
        def sb(stack, name, shape, dt=F32):
            return stack.enter_context(nc.sbuf_tensor(name, shape, dt))

        def sem(name):
            return ctx.enter_context(nc.semaphore(name))

        xt_hi = sb(ctx, "xt_hi", [P, BATCH, KT, SEQ], F32R)
        xt_lo = sb(ctx, "xt_lo", [P, BATCH, KT, SEQ], F32R)
        ident = sb(ctx, "ident", [P, P])
        ident_bf = sb(ctx, "ident_bf", [P, P], BF16)
        mask_q = sb(ctx, "mask_q", [P, SEQ], BF16)
        waited = sb(ctx, "waited", [P, RING])
        mask_k = sb(ctx, "mask_k", [P, P], BF16)
        ones = sb(ctx, "ones", [P, HD])
        eps = sb(ctx, "eps", [P, 1])
        unused = sb(ctx, "unused", [P, 1])
        stats = sb(ctx, "stats", [P, BT, 6])
        mv = sb(ctx, "mv", [P, BT, 2])
        std = sb(ctx, "std", [P, BT])
        rstd = sb(ctx, "rstd", [P, BT])
        x_in = sb(ctx, "x_in", [P, X_SLOTS, HID])

        start = ExitStack()
        with start:
            vo_raw = sb(start, "vo_raw", [P, 2, KT, HID])

        att = ExitStack()
        with att:
            q_stack = sb(att, "q_stack", [P, 2, 2, SEQ], F32R)
            k_stack = sb(att, "k_stack", [P, 2, 2, SEQ], F32R)
            st_hi = sb(att, "st_hi", [P, NCH, CH], F32R)
            st_lo = sb(att, "st_lo", [P, NCH, CH], F32R)
            qk_raw = sb(att, "qk_raw", [P, 2, KT * P + 1])
            qk_hi = sb(att, "qk_hi", [P, 2, KT, P], F32R)
            qk_lo = sb(att, "qk_lo", [P, 2, KT, P], F32R)
            vw_hi = sb(att, "vw_hi", [P, KT, HID], F32R)
            vw_lo = sb(att, "vw_lo", [P, KT, HID], F32R)
            v = sb(att, "v", [P, TT, HID])
            v_pair = sb(att, "v_pair", [P, 2, TT, 2 * HD])
            attn = sb(att, "attn", [P, KT, SEQ])
            outs_sums = sb(att, "outs_sums", [P, 2, CH])
            v_bias = sb(att, "v_bias", [P, HID])
            m_full = sb(att, "m_full", [P, TT, 2])
            m_cols = sb(att, "m_cols", [P, TT, P // HD, HD], F32R)
            ow_hi = sb(att, "ow_hi", [P, KT, HID], F32R)
            ow_lo = sb(att, "ow_lo", [P, KT, HID], F32R)
            o_bias = sb(att, "o_bias", [P, HID])
            probs = sb(att, "probs", [P, 2, 2, CH])
        y, x1 = probs[:, 0], probs[:, 1]
        outs, sums = outs_sums[:, 0], outs_sums[:, 1]
        xn = outs_sums
        ffn = ExitStack()
        with ffn:
            gu_raw = sb(ffn, "gu_raw", [P, 2, KT * GU])
            gu_hi = sb(ffn, "gu_hi", [P, 2, KT * GU], F32R)
            gu_lo = sb(ffn, "gu_lo", [P, 2, KT * GU], F32R)
            dn_raw = sb(ffn, "dn_raw", [P, 2, HID])
            dn_hi = sb(ffn, "dn_hi", [P, 2, HID], F32R)
            dn_lo = sb(ffn, "dn_lo", [P, 2, HID], F32R)
            silu = sb(ffn, "silu", [P, 2, BLK])
            h32 = sb(ffn, "h32", [P, 2, BLK])
            h_hi = sb(ffn, "h_hi", [P, 2, BLK], F32R)
            h_lo = sb(ffn, "h_lo", [P, 2, BLK], F32R)
            acc = sb(ffn, "acc", [P, BT, HID])
            out_t = sb(ffn, "out_t", [P, 2, HID])
        ps = ctx.enter_context(nc.psum_tensor("ps", [P, 8, CH], F32))
        ps_cols = ps.rearrange("p b c -> p (b c)")
        ST_BANK, ACC_BANK = RING, RING + 2
        G_BANK, U_BANK = 4, 6

        consts_loaded = sem("consts_loaded")
        consts_made = sem("consts_made")
        x_loaded = [sem(f"x_loaded{s}") for s in range(X_SLOTS)]
        xn_ready = sem("xn_ready")
        y_ready = sem("y_ready")
        x1_ready = sem("x1_ready")
        x1_stored = [sem(f"x1_stored{s}") for s in range(2)]
        vo_loaded = [sem("vw_loaded"), sem("ow_loaded")]
        vo_hi_done = sem("vo_hi_done")
        vo_split = sem("vo_split")
        qk_loaded = [sem(f"qk_loaded{s}") for s in range(2)]
        qk_split = sem("qk_split")
        pool_hi = sem("pool_hi")
        bank_full = sem("bank_full")
        bank_free = sem("bank_free")
        late_full = sem("late_full")
        late_free = sem("late_free")
        xt_hi_ready = sem("xt_hi_ready")
        st_hi_ready = sem("st_hi_ready")
        v_paired = sem("v_paired")
        stack_loaded = [[sem(f"stack_loaded{s}{c}") for c in range(NCH)] for s in range(2)]
        m_ready = sem("m_ready")
        m_rows0 = sem("m_rows0")
        score_full = sem("score_full")
        p_ready = sem("p_ready")
        p_used = sem("p_used")
        acc_read = sem("acc_read")
        inverted = sem("inverted")
        normalised = sem("normalised")
        attn_split = sem("attn_split")
        attn_hi_ready = sem("attn_hi_ready")
        attn_last_split = sem("attn_last_split")
        var_ready = sem("var_ready")
        std_ready = sem("std_ready")
        dve = sem("dve")
        dve_unit = sem("dve_unit")
        qk_hi_done = sem("qk_hi_done")
        gu_hi_done = sem("gu_hi_done")
        dn_hi_done = sem("dn_hi_done")
        gu_loaded = [sem(f"gu_loaded{s}") for s in range(2)]
        dn_loaded = [sem(f"dn_loaded{s}") for s in range(2)]
        gu_split = sem("gu_split")
        dn_split = sem("dn_split")
        gu_full = sem("gu_full")
        silu_ready = sem("silu_ready")
        h_part = sem("h_part")
        h_ready = sem("h_ready")
        down_done = sem("down_done")
        out_full = sem("out_full")
        acc_out = sem("acc_out")
        out_ready = sem("out_ready")
        out_stored = [sem(f"out_stored{s}") for s in range(2)]

        block = ctx.enter_context(nc.Block())

        @block.sync
        def _(sp):
            sp.dma_start(v_bias[:, :], v_b.partition_broadcast(P)).then_inc(consts_loaded, DMA)
            sp.dma_start(o_bias[:, :], o_b.partition_broadcast(P)).then_inc(consts_loaded, DMA)

            def load_x(n):
                before = n - X_SLOTS
                if before >= 4 * TT:
                    sp.wait_ge(out_ready, before - 4 * TT + 1)
                elif before >= 2 * TT:
                    sp.wait_ge(x1_ready, before - 2 * TT + 1)
                elif before >= 0:
                    sp.wait_ge(xn_ready, before + 1)
                e = n % (2 * TT)
                src = x1_dram if n >= 4 * TT else x
                sp.dma_start(x_in[:, n % X_SLOTS, :], src[e * P:(e + 1) * P, :]).then_inc(x_loaded[n % X_SLOTS], DMA)

            def load_qk(g, i=None):
                if g >= 2:
                    sp.wait_ge(bank_free, at(use_body(g - 2) - PER_UNIT + 1, 2 * PER_UNIT, i))
                u = g % UNITS
                src = qk_w[u] if i is None else qk_w[bass.ds(i * 2 + u, 1)].rearrange("a p n -> (a p) n")
                sp.dma_start(qk_raw[:, g % 2, :], src).then_inc(qk_loaded[g % 2], DMA)

            def load_stack(g, c, i=None):
                s = g % 2
                cols = slice(c * CH, (c + 1) * CH)
                for h in range(2):
                    q, k = slice(h * HD, (h + 1) * HD), slice((2 + h) * HD, (3 + h) * HD)
                    for stack, rows, part in ((q_stack, q, (st_hi, st_lo, st_hi)), (k_stack, k, (st_hi, st_hi, st_lo))):
                        for n, src in enumerate(part):
                            sp.dma_start(stack[n * HD:(n + 1) * HD, s, h, cols].bitcast(F32), src[rows, c, :].bitcast(F32)).then_inc(stack_loaded[s][c], DMA)

            def body(g, i=None):
                if g + 2 < ALL_UNITS:
                    load_qk(g + 2, i)
                if g + 1 < ALL_UNITS:
                    sp.wait_ge(late_free, at(g + 1, 2, i))
                    load_stack(g + 1, 1, i)
                if g + 2 < ALL_UNITS:
                    sp.wait_ge(bank_free, at(use_body(g) + OFF_PROJ + 1, 2 * PER_UNIT, i))
                    load_stack(g + 2, 0, i)

            def residual(b, extra):
                for t in range(X_SLOTS):
                    load_x((2 + b) * TT + t)
                for t in range(TT):
                    e = b * TT + t
                    sp.wait_ge(x1_ready, e + 1)
                    sp.dma_start(x1_dram[e * P:(e + 1) * P, :], x1[:, e % 2, :]).then_inc(x1_stored[e % 2], DMA)
                    if t + X_SLOTS < TT:
                        load_x((2 + b) * TT + t + X_SLOTS)
                    extra(t)

            for n in range(X_SLOTS):
                load_x(n)
                if n == 1:
                    sp.dma_start(vo_raw[:, 0], v_w).then_inc(vo_loaded[0], DMA)
                    load_qk(0)
                    load_qk(1)
            sp.dma_start(vo_raw[:, 1], o_w).then_inc(vo_loaded[1], DMA)
            for n in range(X_SLOTS, TT + X_SLOTS):
                load_x(n)
            sp.wait_ge(vo_split, 1)
            sp.wait_ge(bank_free, use_of_p(0, 0) + 1)
            load_stack(0, 0)
            for n in range(TT + X_SLOTS, 2 * TT):
                load_x(n)
            sp.wait_ge(bank_free, use_of_p(0, 1) + 1)
            load_stack(0, 1)
            sp.wait_ge(vo_split, 2)
            sp.wait_ge(bank_free, use_of_p(1, 0) + 1)
            load_stack(1, 0)
            for b in range(BATCH):
                with sp.Fori(0, UNITS // 2 - 1) as i:
                    for s in range(2):
                        body(b * UNITS + s, i)
                body(b * UNITS + UNITS - 2)
                body(b * UNITS + UNITS - 1)
                if b + 1 < BATCH:
                    residual(b, lambda t: None)

            def of_turn(w, c, i):
                return w[c] if i is None else w[bass.ds(i * 2 + c, 1)].rearrange("a p n -> (a p) n")

            def load_gu(n, c, i=None):
                if n >= 2:
                    sp.wait_ge(gu_split, at(n - 1, 2, i))
                sp.dma_start(gu_raw[:, n % 2], of_turn(gu_w, c, i)).then_inc(gu_loaded[n % 2], DMA)

            def load_dn(n, c, i=None):
                if n >= 2:
                    sp.wait_ge(dn_split, at(n - 1, 2, i))
                sp.dma_start(dn_raw[:, n % 2], of_turn(dn_w, c, i)).then_inc(dn_loaded[n % 2], DMA)

            sp.wait_ge(p_used, NST * (ALL_UNITS - 1))
            for n in range(2):
                load_gu(n, n)

            def first_weights(t):
                for n in range(2):
                    if t == 2:
                        load_dn(n, n)
                    elif t == 5:
                        load_gu(2 + n, 2 + n)

            residual(BATCH - 1, first_weights)
            for s in range(2):
                sp.wait_ge(x1_stored[s], DMA * BATCH * TT // 2)

            def finish(blk):
                for t in range(BT):
                    load_x(2 * BATCH * TT + blk * BT + t)
                for t in range(BT):
                    e = blk * BT + t
                    sp.wait_ge(out_ready, e + 1)
                    sp.dma_start(out[e * P:(e + 1) * P, :], out_t[:, e % 2, :]).then_inc(out_stored[e % 2], DMA)

            for blk in range(BLOCKS):
                n0 = blk * CHUNKS
                for c in range(4):
                    if blk:
                        load_gu(n0 + c, c)
                    if blk or c >= 2:
                        load_dn(n0 + c, c)
                if blk:
                    finish(blk - 1)
                with sp.Fori(0, CHUNKS // 2 - 2) as i:
                    for c in (4, 5):
                        load_gu(n0 + c, c, i)
                        load_dn(n0 + c, c, i)
            finish(BLOCKS - 1)
            for s in range(2):
                sp.wait_ge(out_stored[s], DMA * BLOCKS * BT // 2)

        @block.gpsimd
        def _(pool):
            nc.gpsimd.memset(ident[:, :], 0.0).then_inc(pool_hi, 1)
            nc.gpsimd.memset(mask_q[:, :], 0.0).then_inc(pool_hi, 1)
            nc.gpsimd.memset(mask_k[:, :], 0.0).then_inc(pool_hi, 1)
            nc.gpsimd.memset(ones[:, :], 1.0).then_inc(pool_hi, 1)
            nc.gpsimd.memset(eps[:, :], EPS).then_inc(pool_hi, 1)
            nc.gpsimd.memset(m_cols[:, :, :, :].bitcast(F32), 0.0).then_inc(pool_hi, 1)
            pool.wait_ge(pool_hi, 6)
            nc.gpsimd.affine_select(out=ident[:, :], in_=ident[:, :], compare_op=ALU.not_equal, fill=1.0,
                                    base=0, pattern=[[-1, P]], channel_multiplier=1).then_inc(pool_hi, 1)
            nc.gpsimd.affine_select(out=mask_q[:, SEQ - P:], in_=mask_q[:, SEQ - P:], compare_op=ALU.is_ge, fill=MASKED,
                                    base=0, pattern=[[-1, P]], channel_multiplier=1).then_inc(pool_hi, 1)
            nc.gpsimd.affine_select(out=mask_k[:, :], in_=mask_k[:, :], compare_op=ALU.is_ge, fill=MASKED,
                                    base=0, pattern=[[1, P]], channel_multiplier=-1).then_inc(pool_hi, 1)
            pool.wait_ge(pool_hi, 9)
            nc.gpsimd.tensor_copy(ident_bf[:, :], ident[:, :]).then_inc(consts_made, 1)
            pool.wait_ge(consts_made, 1)
            nc.gpsimd.memset(k_stack[QK_ROWS:ROWS, :, :, :].bitcast(F32), 1.0).then_inc(consts_made, 1)
            pool.wait_ge(consts_made, 2)
            made = [9]

            def split(hi, lo, raw, done):
                nc.gpsimd.tensor_copy(hi, raw).then_inc(pool_hi, 1)
                made[0] += 1
                pool.wait_ge(pool_hi, made[0])
                nc.gpsimd.tensor_tensor(lo, raw, hi.bitcast(F32), ALU.subtract).then_inc(done, 1)

            def qk_rest(g, i=None):
                pool.wait_ge(qk_hi_done, at(g + 1, 2, i))
                nc.gpsimd.tensor_tensor(qk_lo[:, g % 2], qk_raw[:, g % 2, 0:KT * P], qk_hi[:, g % 2].bitcast(F32),
                                        ALU.subtract).then_inc(qk_split, 1)

            def pair_values(g, i=None):
                if g >= 2:
                    pool.wait_ge(p_used, at(NST * (g - 1), 2 * NST, i))
                u = g % UNITS
                cols = bass.ds(i * (4 * HD) + u * 2 * HD, 2 * HD) if i is not None else slice(u * 2 * HD, (u + 1) * 2 * HD)
                nc.gpsimd.tensor_copy(v_pair[:, g % 2], v[:, :, cols]).then_inc(v_paired, 1)

            def gu_rest(n, i=None):
                s = n % 2
                pool.wait_ge(gu_hi_done, at(n + 1, 2, i))
                nc.gpsimd.tensor_tensor(gu_lo[:, s], gu_raw[:, s], gu_hi[:, s].bitcast(F32), ALU.subtract).then_inc(gu_split, 1)

            def dn_rest(n, i=None):
                s = n % 2
                pool.wait_ge(dn_hi_done, at(n + 1, 2, i))
                nc.gpsimd.tensor_tensor(dn_lo[:, s], dn_raw[:, s], dn_hi[:, s].bitcast(F32), ALU.subtract).then_inc(dn_split, 1)

            for n, (hi, lo) in enumerate(((vw_hi, vw_lo), (ow_hi, ow_lo))):
                pool.wait_ge(vo_hi_done, n + 1)
                nc.gpsimd.tensor_tensor(lo[:, :, :], vo_raw[:, n], hi[:, :, :].bitcast(F32), ALU.subtract).then_inc(vo_split, 1)
                if n == 0:
                    qk_rest(0)
                    qk_rest(1)
            for b in range(BATCH):
                g0 = b * UNITS
                if b == 0:
                    pool.wait_ge(bank_free, use_of("V", b, TT - 1) + 1)
                    pair_values(g0)
                with pool.Fori(0, UNITS // 2 - 1) as i:
                    for s in range(2):
                        qk_rest(g0 + s + 2, i)
                        pair_values(g0 + s + 1, i)
                for u in (UNITS - 2, UNITS - 1):
                    if b + 1 < BATCH:
                        qk_rest(g0 + u + 2)
                    if u == UNITS - 2:
                        pair_values(g0 + UNITS - 1)
                pool.wait_ge(late_full, g0 + UNITS - 1)
                for k in range(KT - 1):
                    pool.wait_ge(normalised, NCH * (g0 + 2 * k + 2))
                    split(xt_hi[:, b, k, :], xt_lo[:, b, k, :], attn[:, k, :], attn_split)
                if b + 1 == BATCH:
                    gu_rest(0)
                for t in range(TT):
                    e = b * TT + t
                    n = 2 * TT + e
                    pool.wait_ge(x_loaded[n % X_SLOTS], DMA * (n // X_SLOTS + 1))
                    pool.wait_ge(y_ready, e + 1)
                    if e >= 2:
                        pool.wait_ge(x1_stored[e % 2], DMA * (e // 2))
                        pool.wait_ge(xn_ready, 2 * TT + e - 1)
                    nc.gpsimd.tensor_tensor(x1[:, e % 2, :], x_in[:, n % X_SLOTS, :], y[:, e % 2, :], ALU.add).then_inc(x1_ready, 1)
                    if b + 1 == BATCH and t == 2:
                        gu_rest(1)
                    if b + 1 == BATCH and t == 5:
                        dn_rest(0)
                if b + 1 < BATCH:
                    pool.wait_ge(bank_free, use_of("V", b + 1, TT - 1) + 1)
                    pair_values(g0 + UNITS)
            with pool.Fori(0, BLOCKS * CHUNKS // 2 - 1) as i:
                for s in range(2):
                    gu_rest(s + 2, i)
                    dn_rest(s + 1, i)
            dn_rest(BLOCKS * CHUNKS - 1)

        @block.scalar
        def _(act):
            def root(norms, slot, tiles=1):
                act.wait_ge(var_ready, norms)
                nc.scalar.activation(std[:, slot:slot + tiles], mv[:, slot:slot + tiles, 1], ACT.Sqrt, bias=eps[:, :]).then_inc(std_ready, 1)

            def hi_of_xt(b, t, use):
                act.wait_ge(bank_full, use + 1)
                nc.scalar.activation(xt_hi[:, b, :, t * P:(t + 1) * P], ps[:, use % RING].rearrange("p (k c) -> p k c", k=KT),
                                     ACT.Copy).then_inc(xt_hi_ready, 1)

            def hi_of_proj(g, c, use, i=None):
                if use is None:
                    act.wait_ge(late_full, at(g, 2, i))
                else:
                    act.wait_ge(bank_full, at(use + 1, 2 * PER_UNIT, i))
                bank = ACC_BANK if use is None else use % RING
                if g >= 1:
                    act.wait_ge(stack_loaded[(g - 1) % 2][c], at(DMA * STACK_DMAS * ((g - 1) // 2 + 1), DMA * STACK_DMAS, i))
                nc.scalar.activation(st_hi[:, c, :], ps[:, bank], ACT.Identity, bias=qk_raw[:, g % 2, KT * P:]).then_inc(st_hi_ready, 1)

            def hi_of_vo(n, hi):
                act.wait_ge(vo_loaded[n], DMA)
                nc.scalar.activation(hi[:, :, :], vo_raw[:, n], ACT.Copy).then_inc(vo_hi_done, 1)

            def hi_of_qk(g, i=None):
                s = g % 2
                act.wait_ge(qk_loaded[s], at(DMA * (g // 2 + 1), DMA, i))
                nc.scalar.activation(qk_hi[:, s].rearrange("p k n -> p (k n)"), qk_raw[:, s, 0:KT * P], ACT.Copy).then_inc(qk_hi_done, 1)

            def exps(g, j, i=None):
                c, kt, off = STEPS[j]
                for h in range(2):
                    act.wait_ge(score_full, at(2 * NST * g + 2 * j + h + 1, 4 * NST, i))
                    if g * NST + j >= 2 and h == 0:
                        act.wait_ge(p_used, at(NST * g + j - 1, 2 * NST, i))
                    nc.scalar.activation(probs[:, j % 2, h, 0:CH - off], ps[:, ST_BANK + h, 0:CH - off], ACT.Exp,
                                         scale=SCALE).then_inc(p_ready, 1)

            def copy_acc(g, c, i=None):
                act.wait_ge(p_used, at(NST * g + CHUNK_END[c] + 1, 2 * NST, i))
                if g and c == 0:
                    act.wait_ge(normalised, at(NCH * g, 2 * NCH, i))
                rows = slice(c * 2 * HD, (c + 1) * 2 * HD)
                nc.scalar.activation(outs[rows, :], ps[0:2 * HD, ACC_BANK + c], ACT.Copy).then_inc(acc_read, 1)
                nc.scalar.activation(sums[rows, :], ps[2 * HD:4 * HD, ACC_BANK + c], ACT.Copy).then_inc(acc_read, 1)

            def hi_of_attn(b, c):
                g = (b + 1) * UNITS - 1
                act.wait_ge(late_full, g)
                act.wait_ge(normalised, NCH * g + c + 1)
                cols = slice(c * CH, (c + 1) * CH)
                nc.scalar.activation(xt_hi[:, b, KT - 1, cols], attn[:, KT - 1, cols], ACT.Copy).then_inc(attn_hi_ready, 1)

            def max_rows(g, use, i=None):
                for c in range(NCH):
                    act.wait_ge(bank_full, at(use + c + 1, 2 * PER_UNIT, i))
                    nc.scalar.activation(q_stack[QK_ROWS:ROWS, g % 2, 0, c * CH:(c + 1) * CH], ps[0:2, (use + c) % RING], ACT.Copy).then_inc(m_rows0, 1)

            def body(g, i=None):
                use = use_body(g)
                projected = g + 2 < ALL_UNITS
                for j in range(NST if g >= 0 else 0):
                    exps(g, j, i)
                    if projected and j == 1:
                        hi_of_qk(g + 2, i)
                    if projected and j == STAGE_STEP:
                        hi_of_proj(g + 2, 0, use + OFF_PROJ, i)
                    if j == (COPY_STEP if g < ALL_UNITS - 1 else CHUNK_END[0] + 2):
                        copy_acc(g, 0, i)
                    if g == ALL_UNITS - 1 and j == NST - 2:
                        hi_of_attn(g // UNITS, 0)
                if g >= 0:
                    copy_acc(g, 1, i)
                if g + 1 < ALL_UNITS:
                    max_rows(g + 1, use_max_rows(g), i)
                if projected:
                    hi_of_proj(g + 2, 1, None, i)

            def residual(b, extra):
                lag = LAG_T[b]
                for t in range(TT + lag):
                    if t >= lag:
                        hi_of_xt(b, t - lag, use_of("T", b, t - lag))
                    if t <= TT:
                        slots = range(0 if t < TT else 1, 2 if t else 1)
                        root((2 + 2 * b) * TT + min(2 * t + 1, 2 * TT), slots[0], len(slots))
                    extra(t)

            act.wait_ge(consts_loaded, 2 * DMA)
            act.wait_ge(consts_made, 1)
            for e in range(2 * TT + LAG_X):
                if e < 2 * TT:
                    root(e + 1, e % 2)
                if e >= LAG_X:
                    d = e - LAG_X
                    hi_of_xt(d // TT, d % TT, use_of_xt(d))
                    for g, c in PROJECT_AFTER.get(d, ()):
                        hi_of_proj(g, c, use_of_p(g, c))
                if e == 3:
                    hi_of_vo(0, vw_hi)
                elif e in (4, 5):
                    hi_of_qk(e - 4)
                elif e == 6:
                    hi_of_vo(1, ow_hi)
            body(-1)

            def hi_of_gu(n, i=None):
                s = n % 2
                act.wait_ge(gu_loaded[s], at(DMA * (n // 2 + 1), DMA, i))
                if n >= 2:
                    act.wait_ge(gu_full, at(2 * n - 2, 4, i))
                nc.scalar.activation(gu_hi[:, s], gu_raw[:, s], ACT.Copy).then_inc(gu_hi_done, 1)

            def hi_of_dn(n, i=None):
                s = n % 2
                act.wait_ge(dn_loaded[s], at(DMA * (n // 2 + 1), DMA, i))
                if n >= 2:
                    act.wait_ge(down_done, at(n - 1, 2, i))
                nc.scalar.activation(dn_hi[:, s], dn_raw[:, s], ACT.Copy).then_inc(dn_hi_done, 1)

            def silus(n, i=None):
                s = n % 2
                act.wait_ge(gu_full, at(2 * n + 1, 4, i))
                if n >= 2:
                    act.wait_ge(h_ready, at(n - 1, 2, i))
                nc.scalar.activation(silu[:, s, :], ps[:, G_BANK + s], ACT.Silu).then_inc(silu_ready, 1)

            def first_chunks(t):
                if t == 2:
                    hi_of_gu(1)
                elif t == 5:
                    hi_of_dn(0)
                elif TT <= t < TT + 2:
                    silus(t - TT)

            for b in range(BATCH):
                g0 = b * UNITS
                for s in range(2) if b else ():
                    act.wait_ge(x1_stored[s], DMA * b * TT // 2)
                nc.scalar.activation(unused[:, :], eps[:, :], ACT.Exp)
                with act.Fori(0, UNITS // 2 - 1) as i:
                    for s in range(2):
                        body(g0 + s, i)
                body(g0 + UNITS - 2)
                body(g0 + UNITS - 1)
                for c in range(NCH - 1 if b + 1 == BATCH else 0, NCH):
                    hi_of_attn(b, c)
                if b + 1 == BATCH:
                    hi_of_gu(0)
                residual(b, first_chunks if b + 1 == BATCH else lambda t: None)

            def chunk(n, i=None):
                if n >= 2:
                    silus(n, i)
                if n < BLOCKS * CHUNKS - 2:
                    hi_of_gu(n + 2, i)
                if n < BLOCKS * CHUNKS - 1:
                    hi_of_dn(n + 1, i)

            for blk in range(BLOCKS):
                n0 = blk * CHUNKS
                chunk(n0)
                if blk:
                    root(NORMS + BT * blk, 0, BT)
                chunk(n0 + 1)
                with act.Fori(0, CHUNKS // 2 - 2) as i:
                    chunk(n0 + 2, i)
                    chunk(n0 + 3, i)
                chunk(n0 + CHUNKS - 2)
                chunk(n0 + CHUNKS - 1)
            root(NORMS + BT * BLOCKS, 0, BT)

        @block.vector
        def _(vec):
            n_dve = [0]

            def step(ins):
                n_dve[0] += 1
                ins.then_inc(dve, 1)
                vec.wait_ge(dve, n_dve[0])

            def moments(src, slot):
                step(nc.vector.bn_stats(stats[:, slot, :], src))
                nc.vector.bn_aggr(mv[:, slot, :], stats[:, slot, :]).then_inc(var_ready, 1)

            def centred(dst, src, slot):
                return nc.vector.tensor_scalar(dst, src, mv[:, slot, 0:1], rstd[:, slot:slot + 1], ALU.subtract, ALU.mult)

            def normed(dst, src, n, slot):
                vec.wait_ge(std_ready, n + 1)
                step(nc.vector.reciprocal(rstd[:, slot:slot + 1], std[:, slot:slot + 1]))
                return centred(dst, src, slot)

            tiles_lo = [0]

            def lo_of_xt(b, t, use):
                tiles_lo[0] += 1
                vec.wait_ge(xt_hi_ready, tiles_lo[0])
                cols = slice(t * P, (t + 1) * P)
                nc.vector.tensor_tensor(xt_lo[:, b, :, cols], ps[:, use % RING].rearrange("p (k c) -> p k c", k=KT),
                                        xt_hi[:, b, :, cols].bitcast(F32), ALU.subtract).then_inc(bank_free, 1)

            def lo_of_proj(g, c, use, i=None, banks=2):
                vec.wait_ge(st_hi_ready, at(NCH * g + c + 1, 2 * NCH, i))
                bank, free = (ACC_BANK, late_free) if use is None else (use % RING, bank_free)
                nc.vector.scalar_tensor_tensor(st_lo[:, c, :], ps[:, bank], qk_raw[:, g % 2, KT * P:], st_hi[:, c, :].bitcast(F32),
                                               ALU.add, ALU.subtract).then_inc(free, banks)

            def values(b, t):
                use = use_of("V", b, t)
                vec.wait_ge(bank_full, use + 1)
                if b and t == 0:
                    vec.wait_ge(v_paired, b * UNITS)
                nc.vector.tensor_tensor(v[:, t, :], ps[:, use % RING], v_bias[:, :], ALU.add).then_inc(bank_free, 1)

            def maxima(tiles, use, i=None):
                for n in tiles:
                    h, t, banks = MAXES[n]
                    first = use + MAX_OFF[n]
                    vec.wait_ge(bank_full, at(first + banks, 2 * PER_UNIT, i))
                    scores = ps_cols[:, first % RING * CH:first % RING * CH + (t + 1) * P]
                    nc.vector.tensor_copy(waited[:, first % RING:first % RING + 1], eps[:, :])
                    nc.vector.tensor_tensor_reduce(out=scores, in0=scores, in1=mask_q[:, SEQ - (t + 1) * P:], scale=1.0, scalar=MASKED,
                                                   op0=ALU.add, op1=ALU.max, accum_out=m_full[:, t, h:h + 1]).then_inc(bank_free, banks)

            def negated(g, use, i=None):
                vec.wait_ge(bank_free, at(use, 2 * PER_UNIT, i))
                nc.vector.tensor_scalar(m_cols[:, :, 0:2, 0], m_full[:, :, :], -1.0, None, ALU.mult).then_inc(dve_unit, 1)
                vec.wait_ge(dve_unit, at(g + 1, 2, i))
                nc.vector.scalar_tensor_tensor(m_cols[:, :, 0:2, 1], m_full[:, :, :], -1.0, m_cols[:, :, 0:2, 0].bitcast(F32),
                                               ALU.mult, ALU.subtract).then_inc(m_ready, 1)

            def max_rows(g, use, i=None):
                for c in range(NCH):
                    vec.wait_ge(bank_full, at(use + c + 1, 2 * PER_UNIT, i))
                    vec.wait_ge(m_rows0, at(NCH * g + c + 1, 2 * NCH, i))
                    nc.vector.tensor_copy(q_stack[QK_ROWS:ROWS, g % 2, 1, c * CH:(c + 1) * CH], ps[HD:HD + 2, (use + c) % RING]).then_inc(bank_free, 1)

            def normalise(g, i=None):
                vec.wait_ge(acc_read, at(2 * NCH * (g + 1), 4 * NCH, i))
                nc.vector.reciprocal(sums[:, :], sums[:, :]).then_inc(inverted, 1)
                vec.wait_ge(inverted, at(g + 1, 2, i))
                rows = slice((g % 2) * 2 * HD, (g % 2 + 1) * 2 * HD)
                k = g % UNITS // 2
                for c in range(NCH):
                    part = slice(c * 2 * HD, (c + 1) * 2 * HD)
                    dst = attn[rows, k, c * CH:(c + 1) * CH] if i is None else \
                        attn[rows, bass.ds(i + k, 1), c * CH:(c + 1) * CH].rearrange("p a c -> p (a c)")
                    nc.vector.tensor_tensor(dst, outs[part, :], sums[part, :], ALU.mult).then_inc(normalised, 1)

            def normalise_last(g, c):
                vec.wait_ge(acc_read, 2 * (NCH * g + c + 1))
                part, cols = slice(c * 2 * HD, (c + 1) * 2 * HD), slice(c * CH, (c + 1) * CH)
                step(nc.vector.reciprocal(sums[part, :], sums[part, :]))
                nc.vector.tensor_tensor(attn[(g % 2) * 2 * HD:(g % 2 + 1) * 2 * HD, KT - 1, cols], outs[part, :], sums[part, :], ALU.mult).then_inc(normalised, 1)

            def lo_of_attn(b, c):
                vec.wait_ge(attn_hi_ready, NCH * b + c + 1)
                cols = slice(c * CH, (c + 1) * CH)
                nc.vector.tensor_tensor(xt_lo[:, b, KT - 1, cols], attn[:, KT - 1, cols], xt_hi[:, b, KT - 1, cols].bitcast(F32),
                                        ALU.subtract).then_inc(attn_last_split, 1)

            def body(g, i=None, before=True):
                use = use_body(g)
                projected = g + 2 < ALL_UNITS
                maxima(range(AT_NORM), use, i)
                if before:
                    normalise(g - 1, i)
                maxima(range(AT_NORM, BEFORE), use, i)
                if projected and g >= 0:
                    lo_of_proj(g + 2, 0, use + OFF_PROJ, i)
                late = use_max_rows(g) - BANKS_MAX
                maxima(range(BEFORE, len(MAXES)), late, i)
                negated(g + 1, use_max_rows(g), i)
                max_rows(g + 1, use_max_rows(g), i)
                if projected:
                    lo_of_proj(g + 2, 1, None, i, banks=1)

            def hidden(n, i=None):
                s = n % 2
                vec.wait_ge(silu_ready, at(n + 1, 2, i))
                vec.wait_ge(gu_full, at(2 * n + 2, 4, i))
                nc.vector.tensor_tensor(h32[:, s, :], ps[:, U_BANK + s], silu[:, s, :], ALU.mult).then_inc(h_part, 1)
                vec.wait_ge(h_part, at(2 * n + 1, 4, i))
                if n >= 2:
                    vec.wait_ge(down_done, at(n - 1, 2, i))
                nc.vector.tensor_copy(h_hi[:, s, :], h32[:, s, :]).then_inc(h_part, 1)
                vec.wait_ge(h_part, at(2 * n + 2, 4, i))
                nc.vector.tensor_tensor(h_lo[:, s, :], h32[:, s, :], h_hi[:, s, :].bitcast(F32), ALU.subtract).then_inc(h_ready, 1)

            def residual(b):
                lag = LAG_T[b]
                for t in range(V_STEPS.count(-1) if b + 1 < BATCH else 0):
                    values(b + 1, t)
                for t in range(TT + lag):
                    e, e1 = b * TT + t, b * TT + t - 1
                    first, second = t < TT, 1 <= t <= TT
                    if first:
                        use = use_of("O", b, t)
                        vec.wait_ge(bank_full, use + 1)
                        nc.vector.tensor_tensor(y[:, e % 2, :], ps[:, use % RING], o_bias[:, :], ALU.add).then_inc(bank_free, 1)
                    if t >= lag:
                        lo_of_xt(b, t - lag, use_of("T", b, t - lag))
                    if b + 1 < BATCH and t in V_STEPS:
                        values(b + 1, V_STEPS.index(t))
                    if second:
                        vec.wait_ge(x1_ready, e1 + 1)
                        nc.vector.bn_stats(stats[:, 1, :], x1[:, e1 % 2, :]).then_inc(dve, 1)
                        n_dve[0] += 1
                        second_stats = n_dve[0]
                    if first:
                        vec.wait_ge(bank_free, use + 1)
                        nc.vector.bn_stats(stats[:, 0, :], y[:, e % 2, :]).then_inc(dve, 1)
                        n_dve[0] += 1
                    if second:
                        vec.wait_ge(dve, second_stats)
                        nc.vector.bn_aggr(mv[:, 1, :], stats[:, 1, :]).then_inc(var_ready, 1)
                    if first:
                        vec.wait_ge(dve, n_dve[0])
                        nc.vector.bn_aggr(mv[:, 0, :], stats[:, 0, :]).then_inc(var_ready, 1)
                    if t <= TT:
                        slots = slice(0 if first else 1, 2 if second else 1)
                        vec.wait_ge(std_ready, 2 * TT + b * (TT + 1) + t + 1)
                        step(nc.vector.reciprocal(rstd[:, slots], std[:, slots]))
                    if first:
                        centred(y[:, e % 2, :], y[:, e % 2, :], 0).then_inc(y_ready, 1)
                    if second:
                        centred(xn[:, e1 % 2, :], x1[:, e1 % 2, :], 1).then_inc(xn_ready, 1)
                    if b + 1 == BATCH and t > TT:
                        hidden(t - TT - 1)

            vec.wait_ge(consts_loaded, 2 * DMA)
            vec.wait_ge(consts_made, 1)
            n = 0
            for e in range(2 * TT + LAG_X):
                if e < 2 * TT:
                    vec.wait_ge(x_loaded[e % X_SLOTS], DMA * (e // X_SLOTS + 1))
                    moments(x_in[:, e % X_SLOTS, :], e % 2)
                if 1 <= e <= 2 * TT:
                    d = e - 1
                    normed(xn[:, d % 2, :], x_in[:, d % X_SLOTS, :], d, d % 2).then_inc(xn_ready, 1)
                while e >= LAG_X and n < len(START):
                    kind, t = START[n]
                    n += 1
                    if kind == "X":
                        lo_of_xt(t // TT, t % TT, use_of_xt(t))
                        if t < 2 * TT - 1:
                            break
                    if kind == "V":
                        values(0, t)
                    if kind == "P":
                        lo_of_proj(*t, use_of_p(*t), banks=1 + t[0])
            body(-1, before=False)
            for b in range(BATCH):
                g0 = b * UNITS
                if b:
                    vec.wait_ge(attn_split, (KT - 1) * b)
                body(g0, before=False)
                turns = UNITS // 2 - 1 - b
                with vec.Fori(0, turns) as i:
                    for s in range(2):
                        body(g0 + 1 + s, i)
                for g in range(g0 + 1 + 2 * turns, min(g0 + UNITS, ALL_UNITS - 1)):
                    body(g)
                if b + 1 < BATCH:
                    normalise(g0 + UNITS - 1)
                else:
                    normalise(ALL_UNITS - 2)
                for c in range(NCH):
                    if b + 1 == BATCH:
                        normalise_last(ALL_UNITS - 1, c)
                    lo_of_attn(b, c)
                residual(b)

            def finish(blk):
                final = blk + 1 == BLOCKS
                if not final:
                    vec.wait_ge(down_done, CHUNKS * (blk + 1))
                    for t in range(BT):
                        nc.vector.tensor_copy(acc[:, t, :], ps[:, t]).then_inc(acc_out, 1)
                    vec.wait_ge(acc_out, BT * (blk + 1))
                src = ps if final else acc
                for t in range(BT):
                    if final:
                        vec.wait_ge(out_full, t + 1)
                    step(nc.vector.bn_stats(stats[:, t, :], src[:, t, :]))
                    nc.vector.bn_aggr(mv[:, t, :], stats[:, t, :]).then_inc(var_ready, 1)
                vec.wait_ge(std_ready, ROOTS + blk + 1)
                step(nc.vector.reciprocal(rstd[:, :], std[:, :]))
                for t in range(BT):
                    e = blk * BT + t
                    ex = 2 * BATCH * TT + e
                    step(nc.vector.tensor_scalar(acc[:, t, :], src[:, t, :], mv[:, t, 0:1], rstd[:, t:t + 1], ALU.subtract, ALU.mult))
                    vec.wait_ge(x_loaded[ex % X_SLOTS], DMA * (ex // X_SLOTS + 1))
                    if e >= 2:
                        vec.wait_ge(out_stored[e % 2], DMA * (e // 2))
                    nc.vector.tensor_tensor(out_t[:, e % 2, :], x_in[:, ex % X_SLOTS, :], acc[:, t, :], ALU.add).then_inc(out_ready, 1)

            for blk in range(BLOCKS):
                if blk:
                    hidden(blk * CHUNKS)
                    finish(blk - 1)
                    hidden(blk * CHUNKS + 1)
                with vec.Fori(0, CHUNKS // 2 - 1) as i:
                    hidden(blk * CHUNKS + 2, i)
                    hidden(blk * CHUNKS + 3, i)
            finish(BLOCKS - 1)

        @block.tensor
        def _(pe):
            def three(dst, hi, lo, r_hi, r_lo, start, stop):
                nc.tensor.matmul(dst, hi, r_hi, start=start, stop=False)
                nc.tensor.matmul(dst, hi, r_lo, start=False, stop=False)
                return nc.tensor.matmul(dst, lo, r_hi, start=False, stop=stop)

            def ring(use, i=None):
                if use >= RING:
                    pe.wait_ge(bank_free, at(use - RING + 1, 2 * PER_UNIT, i))
                return ps[:, use % RING]

            def transpose_x(n, use):
                pe.wait_ge(xn_ready, n + 1)
                bank = ring(use)
                for k in range(KT):
                    last = nc.tensor.transpose(bank[:, k * P:(k + 1) * P], xn[:, n % 2, k * P:(k + 1) * P], ident[:, :])
                last.then_inc(bank_full, 1)

            def tokens_by_weights(b, t, hi, lo, use):
                bank = ring(use)
                cols = slice(t * P, (t + 1) * P)
                for k in range(KT):
                    last = three(bank, xt_hi[:, b, k, cols], xt_lo[:, b, k, cols], hi[:, k, :], lo[:, k, :], k == 0, k == KT - 1)
                last.then_inc(bank_full, 1)

            def project(g, b, c, use, i=None, ks=range(KT), banks=2):
                s = g % 2
                if c == 0:
                    pe.wait_ge(qk_split, at(g + 1, 2, i))
                if use is None:
                    if ks[0] == 0 and g >= 2:
                        pe.wait_ge(acc_read, at(2 * NCH * (g - 2) + 2, 4 * NCH, i))
                    bank, full, banks = ps[:, ACC_BANK], late_full, 1
                else:
                    bank, full = ring(use, i), bank_full
                cols = slice(c * CH, (c + 1) * CH)
                for k in ks:
                    last = three(bank, qk_hi[:, s, k, :], qk_lo[:, s, k, :], xt_hi[:, b, k, cols], xt_lo[:, b, k, cols],
                                 k == 0, k == KT - 1)
                if ks[-1] == KT - 1:
                    last.then_inc(full, banks)

            def first_pass(g, n, use, i=None):
                s = g % 2
                if n in (0, EARLY):
                    pe.wait_ge(stack_loaded[s][0 if n == 0 else 1], at(DMA * STACK_DMAS * (g // 2 + 1), DMA * STACK_DMAS, i))
                h, t, banks = MAXES[n]
                ring(use + banks - 1, i)
                for half in range(banks):
                    bank = ps[:, (use + half) % RING]
                    width = min(CH, (t + 1) * P - half * CH)
                    last = nc.tensor.matmul(bank[:, 0:width], q_stack[0:QK_ROWS, s, h, t * P:(t + 1) * P],
                                            k_stack[0:QK_ROWS, s, h, half * CH:half * CH + width], start=True, stop=True)
                last.then_inc(bank_full, banks)

            def transpose_maxima(g, use, i=None):
                pe.wait_ge(m_ready, at(g + 1, 2, i))
                for c in range(NCH):
                    bank = ring(use + c, i)
                    for t in range(CH // P):
                        cols = m_cols[:, c * CH // P + t].rearrange("p h n -> p (h n)").bitcast(F32)
                        last = nc.tensor.transpose(bank[:, t * P:(t + 1) * P], cols, ident[:, :])
                    last.then_inc(bank_full, 1)

            def scores(g, j, i=None):
                s = g % 2
                c, kt, off = STEPS[j]
                if kt == 0:
                    pe.wait_ge(bank_free, at(use_body(g) - NCH + c + 1, 2 * PER_UNIT, i))
                diagonal = kt * P >= c * CH
                n = 2 * (NST * g + j)
                for h in range(2):
                    if n + h >= 2:
                        pe.wait_ge(p_ready, at(n + h - 1, 4 * NST, i))
                    bank = ps[:, ST_BANK + h]
                    last = nc.tensor.matmul(bank[:, 0:CH - off], k_stack[0:ROWS, s, h, kt * P:(kt + 1) * P],
                                            q_stack[0:ROWS, s, h, c * CH + off:(c + 1) * CH], start=True, stop=not diagonal)
                    if diagonal:
                        last = nc.tensor.matmul(bank[:, 0:P], ident_bf[:, :], mask_k[:, :], start=False, stop=True)
                    last.then_inc(score_full, 1)

            def values(g, j, i=None):
                s = g % 2
                c, kt, off = STEPS[j]
                if kt == 0 and g >= 1:
                    pe.wait_ge(acc_read, at(2 * (NCH * (g - 1) + c + 1), 4 * NCH, i))
                if j == 0 and g + 1 < ALL_UNITS:
                    pe.wait_ge(late_free, at(g + 1, 2, i))
                pe.wait_ge(p_ready, at(2 * (NST * g + j) + 2, 4 * NST, i))
                for n in range(4):
                    lhs = v_pair[:, s, kt, n * HD:(n + 1) * HD] if n < 2 else ones[:, :]
                    last = nc.tensor.matmul(ps[n * HD:(n + 1) * HD, ACC_BANK + c, off:CH], lhs, probs[:, j % 2, n % 2, 0:CH - off],
                                            start=kt == 0, stop=j == CHUNK_END[c])
                last.then_inc(p_used, 1)

            def body(g, i=None):
                use = use_body(g)
                ahead, projected = g + 1 < ALL_UNITS, g + 2 < ALL_UNITS
                batch = (g + 2) // UNITS
                if g >= 0:
                    pe.wait_ge(v_paired, at(g + 1, 2, i))
                    scores(g, 0, i)
                late = 0
                n = 0
                for j in range(NST):
                    if g >= 0 and 0 < j < NST - 1:
                        scores(g, j + 1, i)
                    while ahead and n < DONE[j]:
                        first_pass(g + 1, n, use + late + MAX_OFF[n], i)
                        n += 1
                    if projected and g >= 0 and j == PROJECT_STEP:
                        project(g + 2, batch, 0, use + OFF_PROJ, i)
                        late = 2
                    if g >= 0 and j == 0:
                        scores(g, 1, i)
                    if g >= 0:
                        values(g, j, i)
                if projected:
                    project(g + 2, batch, 1, None, i, range(0, SPLIT_K))
                if ahead:
                    transpose_maxima(g + 1, use_max_rows(g), i)
                if projected:
                    project(g + 2, batch, 1, None, i, range(SPLIT_K, KT))

            def residual(b, order, extra):
                for n, (kind, t) in enumerate(order):
                    if kind == "V":
                        tokens_by_weights(b + 1, t, vw_hi, vw_lo, use_of("V", b + 1, t))
                    elif kind == "O":
                        if t == 0:
                            pe.wait_ge(attn_split, (KT - 1) * (b + 1))
                        if t % (TT // NCH) == 0:
                            pe.wait_ge(attn_last_split, NCH * b + t // (TT // NCH) + 1)
                        tokens_by_weights(b, t, ow_hi, ow_lo, use_of("O", b, t))
                    else:
                        transpose_x(2 * TT + b * TT + t, use_of("T", b, t))
                    extra(kind, t)

            def gate_and_up(blk, n, i=None):
                s = n % 2
                b, cols = blk * BLK // SEQ, slice(blk * BLK % SEQ, blk * BLK % SEQ + BLK)
                pe.wait_ge(gu_split, at(n + 1, 2, i))
                if n >= 2:
                    pe.wait_ge(h_ready, at(n - 1, 2, i))
                for part, bank in enumerate((G_BANK, U_BANK)):
                    for k in range(KT):
                        w = slice(k * GU + part * P, k * GU + (part + 1) * P)
                        last = three(ps[:, bank + s], gu_hi[:, s, w], gu_lo[:, s, w], xt_hi[:, b, k, cols], xt_lo[:, b, k, cols], k == 0, k == KT - 1)
                    last.then_inc(gu_full, 1)

            def down(blk, n, first, final, i=None):
                s = n % 2
                pe.wait_ge(h_ready, at(n + 1, 2, i))
                pe.wait_ge(dn_split, at(n + 1, 2, i))
                for t in range(BT):
                    if first and blk:
                        pe.wait_ge(acc_out, BT * (blk - 1) + t + 1)
                    cols = slice(t * P, (t + 1) * P)
                    last = three(ps[:, t], h_hi[:, s, cols], h_lo[:, s, cols], dn_hi[:, s], dn_lo[:, s], first, final)
                    if n == BLOCKS * CHUNKS - 1:
                        last.then_inc(out_full, 1)
                if n < BLOCKS * CHUNKS - 1:
                    last.then_inc(down_done, 1)

            def first_chunks(kind, t):
                if (kind, t) in FIRST_CHUNKS:
                    pe.wait_ge(acc_read, 2 * NCH * ALL_UNITS)
                    gate_and_up(0, FIRST_CHUNKS.index((kind, t)))

            pe.wait_ge(consts_made, 1)
            for kind, t in START:
                if kind == "X":
                    transpose_x(t, use_of_xt(t))
                elif kind == "V":
                    if t == 0:
                        pe.wait_ge(vo_split, 1)
                    pe.wait_ge(bank_free, use_of_xt(t) + 1)
                    tokens_by_weights(0, t, vw_hi, vw_lo, use_of("V", 0, t))
                elif kind == "P":
                    pe.wait_ge(bank_free, use_of_xt(TT - 1) + 1)
                    project(t[0], 0, t[1], use_of_p(*t), banks=1 + t[0])
            pe.wait_ge(consts_made, 2)
            body(-1)
            pe.wait_ge(vo_split, 2)
            for b in range(BATCH):
                g0 = b * UNITS
                with pe.Fori(0, UNITS // 2 - 1) as i:
                    for s in range(2):
                        body(g0 + s, i)
                body(g0 + UNITS - 2)
                body(g0 + UNITS - 1)
                if b + 1 < BATCH:
                    residual(b, MID, lambda kind, t: None)
                else:
                    residual(b, END, first_chunks)

            pe.wait_ge(bank_free, USES)
            for blk in range(BLOCKS):
                n0 = blk * CHUNKS
                if blk:
                    gate_and_up(blk, n0 + 1)
                down(blk, n0, True, False)
                with pe.Fori(0, CHUNKS // 2 - 1) as i:
                    for s in range(2):
                        gate_and_up(blk, n0 + 2 + s, i)
                        down(blk, n0 + 1 + s, False, False, i)
                if blk + 1 < BLOCKS:
                    gate_and_up(blk + 1, n0 + CHUNKS)
                down(blk, n0 + CHUNKS - 1, False, True)


def kernel(**inputs):
    import numpy as _np
    import concourse.bacc as _bacc
    from concourse import mybir as _mybir
    from concourse.bass_utils import run_bass_kernel_spmd as _run

    a = {k.removeprefix("L0_"): _np.asarray(v) for k, v in inputs.items()}
    pairs = _np.stack([a["attn_q_w"].reshape(UNITS, 2 * HD, HID), a["attn_k_w"].reshape(UNITS, 2 * HD, HID)], 1)
    bias = _np.stack([a["attn_q_b"].reshape(UNITS, 2 * HD), a["attn_k_b"].reshape(UNITS, 2 * HD)], 1).reshape(UNITS, P, 1)
    gate, up = a["ffn_w_gate_up"].reshape(2, CHUNKS, P, KT, P)
    gu = _np.stack([gate, up], 1).transpose(0, 4, 3, 1, 2).reshape(CHUNKS, P, KT * GU)
    dn = a["ffn_w_down"].reshape(HID, CHUNKS, P).transpose(1, 2, 0)
    arrays = {
        "x": a["attn_hidden_states"].reshape(BATCH * SEQ, HID),
        "qk_w": _np.concatenate([pairs.reshape(UNITS, P, KT, P).transpose(0, 3, 2, 1).reshape(UNITS, P, KT * P), bias], 2),
        "v_w": a["attn_v_w"].reshape(HID, KT, P).transpose(2, 1, 0),
        "o_w": a["attn_o_w"].reshape(HID, KT, P).transpose(2, 1, 0),
        "v_b": a["attn_v_b"],
        "o_b": a["attn_o_b"],
        "gu_w": gu,
        "dn_w": dn,
    }
    arrays = {k: _np.ascontiguousarray(v) for k, v in arrays.items()}
    nc = _bacc.Bacc("TRN2", target_bir_lowering=False, num_devices=1, dynamic_dma_scratch_size=1024)
    args = [nc.dram_tensor(k, v.shape, _mybir.dt.from_np(v.dtype), kind="ExternalInput").ap() for k, v in arrays.items()]
    x1 = nc.dram_tensor("x1_dram", (BATCH * SEQ, HID), _mybir.dt.float32, kind="Internal").ap()
    out = nc.dram_tensor("out", (BATCH * SEQ, HID), _mybir.dt.float32, kind="ExternalOutput").ap()
    build(nc, *args, x1, out)
    r = _run(nc, [arrays], core_ids=[0])
    return r.results[0]["out"].reshape(BATCH, SEQ, HID)
```
